# Optimizing a Trainium2 kernel written in Bass

```python
import numpy as np
import jax
import jax.numpy as jnp

def _softmax(x, axis=-1):
    return jax.nn.softmax(x, axis=axis)

def _gelu(x):
    return jax.nn.gelu(x, approximate=True)

def _silu(x):
    return jax.nn.silu(x)

def _sigmoid(x):
    return jax.nn.sigmoid(x)

def _layernorm(x, axis=-1, eps=1e-05):
    m = jnp.mean(x, axis=axis, keepdims=True)
    v = jnp.var(x, axis=axis, keepdims=True)
    return (x - m) / jnp.sqrt(v + eps)

def _scatter_add(tgt, idx, src, axis=0):
    return tgt.at[idx].add(src)

def _segment_sum(src, seg, n):
    return jax.ops.segment_sum(src, seg, n)
kernel_name = 'mk_sandwich_d1_jaxref_r8_41a33e'

def setup_inputs(seed: int=0):
    np.random.seed(seed)
    _w = jnp.asarray

    def _L0_attn_setup():
        import jax, jax.numpy as jnp
        import numpy as np
        DIM = 128

        def _circ_conv(x, key):
            D = x.shape[-1]
            return jnp.fft.irfft(jnp.fft.rfft(x, axis=-1) * jnp.fft.rfft(key), n=D, axis=-1)

        def _circ_corr(x, key):
            D = x.shape[-1]
            return jnp.fft.irfft(jnp.fft.rfft(x, axis=-1) * jnp.conj(jnp.fft.rfft(key)), n=D, axis=-1)
        key = jax.random.key(seed)
        k0, k1, k2 = jax.random.split(key, 3)
        B, T, D = (4, 256, DIM)
        x = jax.random.normal(k0, (B, T, D), dtype=jnp.float32)
        bind_key = jax.random.normal(k1, (D,), dtype=jnp.float32) * 0.02
        unbind_key = jax.random.normal(k2, (D,), dtype=jnp.float32) * 0.02
        gate = jnp.ones((1,), dtype=jnp.float32)
        decay = jnp.asarray(0.9, dtype=jnp.float32)
        return {'x': x, 'bind_key': bind_key, 'unbind_key': unbind_key, 'gate': gate, 'decay': decay}
    _L0_attn_in = _L0_attn_setup()

    def _L0_ffn_setup():
        import jax, jax.numpy as jnp
        import numpy as np
        S, B, H, F, E, K = (256, 4, 128, 512, 8, 2)
        key = jax.random.key(seed)
        k1, k2, k3, k4 = jax.random.split(key, 4)
        scale_h = 1.0 / np.sqrt(H)
        scale_f = 1.0 / np.sqrt(F)
        return {'x': jax.random.normal(k1, (S, B, H), dtype=jnp.float32), 'router_w': jax.random.normal(k2, (H, E), dtype=jnp.float32) * scale_h, 'w1': jax.random.normal(k3, (E, H, F), dtype=jnp.float32) * scale_h, 'w2': jax.random.normal(k4, (E, F, H), dtype=jnp.float32) * scale_f}
    _L0_ffn_in = _L0_ffn_setup()
    _d = {'L0_attn_x': _L0_attn_in['x'], 'L0_attn_bind_key': _L0_attn_in['bind_key'], 'L0_attn_unbind_key': _L0_attn_in['unbind_key'], 'L0_attn_gate': _L0_attn_in['gate'], 'L0_attn_decay': _L0_attn_in['decay'], 'L0_ffn_router_w': _L0_ffn_in['router_w'], 'L0_ffn_w1': _L0_ffn_in['w1'], 'L0_ffn_w2': _L0_ffn_in['w2']}
    _x0 = _d['L0_attn_x']
    _d['L0_attn_x'] = jax.random.normal(jax.random.fold_in(jax.random.key(seed), 1), (4, 512, 128), dtype=_x0.dtype)
    del _x0
    return _d

def reference(L0_attn_x, L0_attn_bind_key, L0_attn_unbind_key, L0_attn_gate, L0_attn_decay, L0_ffn_router_w, L0_ffn_w1, L0_ffn_w2):

    def _L0_attn_ref(x, bind_key, unbind_key, gate, decay):
        import jax, jax.numpy as jnp
        import numpy as np
        DIM = 128

        def _circ_conv(x, key):
            D = x.shape[-1]
            return jnp.fft.irfft(jnp.fft.rfft(x, axis=-1) * jnp.fft.rfft(key), n=D, axis=-1)

        def _circ_corr(x, key):
            D = x.shape[-1]
            return jnp.fft.irfft(jnp.fft.rfft(x, axis=-1) * jnp.conj(jnp.fft.rfft(key)), n=D, axis=-1)
        B, T, D = x.shape
        bound = _circ_conv(x, bind_key)
        d = jax.nn.sigmoid(decay)
        pos = jnp.arange(T, dtype=x.dtype)
        diff = pos[:, None] - pos[None, :]
        causal = diff >= 0
        decay_matrix = jnp.where(causal, d ** jnp.maximum(diff, 0.0), 0.0)
        hologram = jnp.einsum('ts,bsd->btd', decay_matrix, bound)
        retrieved = _circ_corr(hologram, unbind_key)
        return x + gate * retrieved

    def _L0_ffn_ref(x, router_w, w1, w2):
        import jax, jax.numpy as jnp
        import numpy as np
        S, B, H, F, E, K = (256, 4, 128, 512, 8, 2)
        s, b, h = x.shape
        xt = x.reshape(-1, h)
        logits = xt @ router_w
        probs = jax.nn.softmax(logits, axis=-1)
        top_p, top_i = jax.lax.top_k(probs, K)
        out = jnp.zeros_like(xt)
        for e in range(E):
            gate_e = jnp.sum(jnp.where(top_i == e, top_p, 0.0), axis=-1)
            hidden = jax.nn.gelu(xt @ w1[e], approximate=True)
            out = out + gate_e[:, None] * (hidden @ w2[e])
        return out.reshape(s, b, h)
    x = L0_attn_x
    x = x + _layernorm(_L0_attn_ref(_layernorm(x, axis=-1), L0_attn_bind_key, L0_attn_unbind_key, L0_attn_gate, L0_attn_decay), axis=-1)
    x = x + _layernorm(_L0_ffn_ref(_layernorm(x, axis=-1), L0_ffn_router_w, L0_ffn_w1, L0_ffn_w2), axis=-1)
    return x

_drawn_inputs = setup_inputs


def setup_inputs(seed=0):
    import zlib

    import numpy as np

    out = dict(_drawn_inputs(seed))
    spreads = {}
    factors = {}
    for name, (base, spread) in spreads.items():
        noise = np.random.default_rng([zlib.crc32(name.encode()), seed]).standard_normal(out[name].shape)
        drawn = base * np.exp(spread * noise) if base else spread * noise
        out[name] = jnp.asarray(drawn.astype(out[name].dtype))
    for name, factor in factors.items():
        out[name] = (out[name] * factor).astype(out[name].dtype)
    return out
```

```python
from contextlib import ExitStack

import concourse.bass as bass
from concourse import mybir

P = 128
D = 128
SEQS, SEQ = 4, 512
TOKENS = SEQS * SEQ
TILES = TOKENS // P
CHUNKS = SEQ // P
HALVES = 2
HT = TILES // HALVES
HS = SEQS // HALVES
E, F, K = 8, 512, 2
FC = F // P
EPS = 1e-5

REGION = TOKENS + P
FULL_BLOCKS = K * TOKENS // P
BLOCKS = 40
assert BLOCKS >= (K * TOKENS + E * (P - 1)) // P
SPARE = BLOCKS - FULL_BLOCKS
ROW = D + 2
ADDR, GATE = D, D + 1
RING = 4

F32 = mybir.dt.float32
I32 = mybir.dt.int32
BF16 = mybir.dt.bfloat16
ALU = mybir.AluOpType
ACT = mybir.ActivationFunctionType
AX = mybir.AxisListType


def build(nc, x_in, keys_in, scalars_in, router_in, w1_in, w2_in, out, slots, returned):
    ctx = ExitStack()
    with ctx:
        def sb(name, shape, dt=F32):
            return ctx.enter_context(nc.sbuf_tensor(name, shape, dt))

        def sem(name):
            return ctx.enter_context(nc.semaphore(name))

        x = sb("x", [P, TILES, D])
        x1 = sb("x1", [P, TILES, D])
        w1 = sb("w1", [P, E, F])
        w2 = sb("w2", [P, E, FC, D])
        router = sb("router", [P, E])
        rows = sb("rows", [P, TILES, K, ROW])
        slot_of = sb("slot_of", [P, K, TILES], I32)
        ident = sb("ident", [P, P])
        below = sb("below", [P, P], BF16)
        ones = sb("ones", [P, P], BF16)
        minus_half = sb("minus_half", [P, HT])
        prefer = sb("prefer", [P, HT, E])
        region_row = sb("region_row", [P, E])
        step_no = sb("step_no", [P, BLOCKS])
        pads = sb("pads", [P, E + SPARE, ROW])
        scalars = sb("scalars", [P, 2])
        hankel = sb("hankel", [P, 2, P])
        mix = sb("mix", [P, P])
        dpow = sb("dpow", [P, 9])
        dtmp = sb("dtmp", [P, 2])
        W2P = 2 * P
        toep = [sb(f"toep{i}", [P, P + W2P]) for i in range(2)]
        decay_m = sb("decay_m", [P, SEQ])
        st = sb("st", [P, HT, 6])
        mv = [sb(f"mv{i}", [P, HT, 2]) for i in range(3)]
        ve = [sb(f"ve{i}", [P, HT]) for i in range(3)]
        rstd = [sb(f"rstd{i}", [P, HT]) for i in range(3)]
        n1 = sb("n1", [P, HT, D])
        holo_t = sb("holo_t", [P, HS, SEQ])
        mixed = sb("mixed", [P, HT, D])
        normed = sb("normed", [P, HT, D])
        n3 = sb("n3", [P, HT, D])
        n3_t = sb("n3_t", [P, HS, SEQ])
        lmax = sb("lmax", [P, HT])
        lg = sb("lg", [P, HT, E])
        ex = sb("ex", [P, HT, E])
        esum = sb("esum", [P, HT])
        einv = sb("einv", [P, HT])
        prob = sb("prob", [P, HT, E])
        rest = sb("rest", [P, HT, E])
        top = [sb(f"top{k}", [P, HT]) for k in range(K)]
        tied = sb("tied", [P, HT, E])
        ranked = sb("ranked", [P, HT, E])
        best = sb("best", [P, HT])
        pick = [sb(f"pick{k}", [P, HT, E]) for k in range(K)]
        picks = sb("picks", [P, HT, E], BF16)
        count = sb("count", [P, E])
        base = sb("base", [P, E])
        place = sb("place", [P, HT, E])
        chosen = sb("chosen", [P, HT, E])
        slotf = sb("slotf", [P, HT])
        pad_row = sb("pad_row", [P, E], I32)
        cnt_i = sb("cnt_i", [P, E], I32)
        nblk_i = sb("nblk_i", [P, E], I32)
        nblk = sb("nblk", [P, E])
        cum = [sb(f"cum{i}", [P, 4 + E]) for i in range(2)]
        past = sb("past", [P, BLOCKS, E])
        pastn = sb("pastn", [P, BLOCKS, E])
        be = sb("be", [P, BLOCKS])
        bn = sb("bn", [P, BLOCKS])
        bt = sb("bt", [P, BLOCKS])
        block_expert = sb("block_expert", [P, BLOCKS], I32)
        block_row = sb("block_row", [P, BLOCKS], I32)
        xg = [sb(f"xg{i}", [P, ROW]) for i in range(RING)]
        xg_t = [sb(f"xg_t{i}", [P, P]) for i in range(2)]
        hid = [sb(f"hid{i}", [P, F]) for i in range(2)]
        hid_t = [sb(f"hid_t{i}", [P, FC, P]) for i in range(2)]
        y = [sb(f"y{i}", [P, D]) for i in range(RING)]
        yk = sb("yk", [P, TILES, K * D])
        ff = sb("ff", [P, TILES, D])
        fst = sb("fst", [P, TILES, 6])
        fmv = sb("fmv", [P, TILES, 2])
        fve = sb("fve", [P, TILES])
        frstd = sb("frstd", [P, TILES])
        fn = sb("fn", [P, TILES, D])
        fo = sb("fo", [P, TILES, D])

        bank = [ctx.enter_context(nc.psum_tensor(f"bank{i}", [P, 512], F32)) for i in range(8)]
        holo_ps, ret_ps, n3t_ps = bank[0:2], bank[2:4], bank[4:6]
        logit_ps = bank[6][:, 0:HT * E].rearrange("p (u e) -> p u e", e=E)
        mix_ps = bank[6][:, 0:P]
        rank_ps = bank[7][:, 0:HT * E].rearrange("p (u e) -> p u e", e=E)
        total_ps = bank[7][:, HT * E:HT * E + E]
        xgt_ps, up_ps, hidt_ps, y_ps = bank[0:2], bank[2:4], bank[4:6], bank[6:8]

        scalars_loaded = sem("scalars_loaded")
        keys_loaded = sem("keys_loaded")
        x_loaded = sem("x_loaded")
        router_loaded = sem("router_loaded")
        w1_loaded = sem("w1_loaded")
        w2_loaded = sem("w2_loaded")
        consts = sem("consts")
        consts_step = sem("consts_step")
        sig = sem("sig")
        dexp_done = sem("dexp_done")
        dpow_done = sem("dpow_done")
        toep_done = sem("toep_done")
        decay_m_done = sem("decay_m_done")
        mix_mm = sem("mix_mm")
        mix_done = sem("mix_done")
        stats_done = [sem(f"stats_done{i}") for i in range(3)]
        aggr_done = [sem(f"aggr_done{i}") for i in range(3)]
        eps_added = [sem(f"eps_added{i}") for i in range(3)]
        rstd_done = [sem(f"rstd_done{i}") for i in range(3)]
        n1_done = sem("n1_done")
        holo_mm = sem("holo_mm")
        holo_out = sem("holo_out")
        ret_mm = sem("ret_mm")
        mixed_done = sem("mixed_done")
        normed_done = sem("normed_done")
        x1_done = sem("x1_done")
        n3_done = sem("n3_done")
        n3t_mm = sem("n3t_mm")
        n3t_out = sem("n3t_out")
        rows_copied = sem("rows_copied")
        logits_mm = sem("logits_mm")
        lsub_done = sem("lsub_done")
        exp_done = sem("exp_done")
        picks_done = sem("picks_done")
        rank_mm = sem("rank_mm")
        router_step = sem("router_step")
        chosen_done = sem("chosen_done")
        slotf_done = sem("slotf_done")
        slots_done = sem("slots_done")
        gates_done = sem("gates_done")
        dispatched = sem("dispatched")
        pads_ready = sem("pads_ready")
        spare_padded = sem("spare_padded")
        padded = sem("padded")
        pad_rows_done = sem("pad_rows_done")
        table_step = sem("table_step")
        table_done = sem("table_done")
        xg_loaded = [sem(f"xg_loaded{i}") for i in range(RING)]
        xgt_mm = sem("xgt_mm")
        xgt_out = sem("xgt_out")
        up_mm = sem("up_mm")
        gelu_done = sem("gelu_done")
        hidt_mm = sem("hidt_mm")
        hidt_out = sem("hidt_out")
        down_mm = sem("down_mm")
        y_done = sem("y_done")
        sends = sem("sends")
        aggregations = sem("aggregations")
        y_sent = [sem(f"y_sent{i}") for i in range(RING)]
        yk_loaded = [sem(f"yk_loaded{i}") for i in range(SEQS)]
        ff_done = sem("ff_done")
        fstats_done = sem("fstats_done")
        faggr_done = sem("faggr_done")
        feps_done = sem("feps_done")
        frstd_done = sem("frstd_done")
        fn_done = sem("fn_done")
        fo_done = sem("fo_done")
        stored = sem("stored")

        block = ctx.enter_context(nc.Block())
        x_tiles = x_in.rearrange("s (c p) d -> s p c d", p=P)
        out_tiles = out.rearrange("s (c p) d -> s p c d", p=P)

        @block.sync
        def _(sp):
            sp.dma_start(scalars[:], scalars_in).then_inc(scalars_loaded, 16)
            for s in range(SEQS):
                sp.dma_start(x[:, CHUNKS * s:CHUNKS * (s + 1), :], x_tiles[s]).then_inc(x_loaded, 16)
            for k in range(2):
                sp.dma_start(hankel[:, k, :], bass.AP(keys_in.tensor, 2 * P * k, [[1, P], [1, P]])) \
                    .then_inc(keys_loaded, 16)
            sp.dma_start(router[:], router_in).then_inc(router_loaded, 16)
            sp.wait_ge(pads_ready, 2)
            sp.dma_start(slots[E * REGION:E * REGION + SPARE * P, :].rearrange("(b p) c -> p b c", p=P),
                         pads[:, E:, :]).then_inc(spare_padded, 16)
            sp.wait_ge(pad_rows_done, 1)
            for e in range(E):
                first = sp.value_load(pad_row[0:1, e:e + 1], min_val=0, max_val=E * REGION - P)
                sp.dma_start(slots[bass.ds(first, P), :], pads[:, e, :]).then_inc(padded, 16)
            sp.wait_ge(spare_padded, 16)
            sp.wait_ge(padded, 16 * E)
            sp.wait_ge(dispatched, 16 * TILES * K)
            sp.wait_ge(table_done, 2)

            def load_block(i, j, first_round):
                row = sp.value_load(block_row[0:1, bass.ds(i, 1)], min_val=0,
                                    max_val=E * REGION + (SPARE - 1) * P)
                if not first_round:
                    sp.wait_ge(y_sent[j], i * (16 // RING) - j * (16 // RING))
                sp.dma_start(xg[j][:], slots[bass.ds(row, P), :]).then_inc(xg_loaded[j], 16)

            for j in range(RING):
                load_block(j, j, True)
            with sp.Fori(1, BLOCKS // RING) as r:
                for j in range(RING):
                    load_block(r * RING + j, j, False)
            for j in range(RING):
                sp.wait_ge(y_sent[j], 16 * BLOCKS // RING)
            back = returned[0:K * TOKENS, :].rearrange("(s c p k) d -> s p c (k d)", c=CHUNKS, p=P, k=K)
            for s in range(SEQS):
                sp.dma_start(yk[:, CHUNKS * s:CHUNKS * (s + 1), :], back[s]).then_inc(yk_loaded[s], 16)
            for s in range(SEQS):
                sp.wait_ge(fo_done, s + 1)
                sp.dma_start(out_tiles[s], fo[:, CHUNKS * s:CHUNKS * (s + 1), :]).then_inc(stored, 16)
            sp.wait_ge(stored, 16 * SEQS)

        @block.gpsimd
        def _(pool):
            pool.memset(toep[0][:], 0.0).then_inc(consts_step, 1)
            pool.memset(ident[:], 0.0).then_inc(consts_step, 1)
            pool.memset(minus_half[:], -0.5).then_inc(consts, 1)
            pool.wait_ge(consts_step, 2)
            pool.affine_select(out=toep[0][:, P:], in_=toep[0][:, P:], compare_op=ALU.not_equal, fill=1.0, base=0,
                               pattern=[[-1, W2P]], channel_multiplier=1).then_inc(consts, 1)
            pool.memset(toep[1][:, 0:P], 0.0).then_inc(consts, 1)
            pool.affine_select(out=ident[:], in_=ident[:], compare_op=ALU.not_equal, fill=1.0, base=0,
                               pattern=[[-1, P]], channel_multiplier=1).then_inc(consts, 1)

            pool.wait_ge(sig, 3)
            for b in range(8):
                if b:
                    pool.wait_ge(dpow_done, b)
                pool.tensor_tensor(out=dpow[:, b + 1:b + 2], in0=dpow[:, b:b + 1], in1=dpow[:, b:b + 1],
                                   op=ALU.mult).then_inc(dpow_done, 1)

            def one_over_std(h, n):
                pool.wait_ge(aggr_done[n], HT * (h + 1))
                pool.tensor_scalar(ve[n][:], mv[n][:, :, 1], EPS, 1.0, ALU.add, ALU.mult).then_inc(eps_added[n], 1)
                pool.wait_ge(eps_added[n], h + 1)
                pool.tensor_tensor(out=rstd[n][:], in0=ve[n][:], in1=minus_half[:], op=ALU.pow) \
                    .then_inc(rstd_done[n], 1)

            one_over_std(0, 0)
            pool.memset(below[:], 1.0).then_inc(consts_step, 1)
            pool.memset(ones[:], 1.0).then_inc(consts, 1)
            pool.wait_ge(consts_step, 3)
            pool.affine_select(out=below[:], in_=below[:], compare_op=ALU.is_gt, fill=0.0, base=0,
                               pattern=[[1, P]], channel_multiplier=-1).then_inc(consts, 1)
            pool.iota(prefer[:], pattern=[[0, HT], [-1, E]], base=E, channel_multiplier=0,
                      allow_small_or_imprecise_dtypes=True).then_inc(consts, 1)
            pool.iota(region_row[:], pattern=[[REGION, E]], base=0, channel_multiplier=0,
                      allow_small_or_imprecise_dtypes=True).then_inc(consts, 1)
            pool.iota(step_no[:], pattern=[[1, BLOCKS]], base=0, channel_multiplier=0,
                      allow_small_or_imprecise_dtypes=True).then_inc(consts, 1)
            pool.memset(count[:], 0.0).then_inc(consts, 1)
            for c in range(2):
                pool.memset(cum[c][:], 0.0).then_inc(consts, 1)
            pool.iota(rows[:, :, :, ADDR].bitcast(I32), pattern=[[K * P, TILES], [1, K]], base=0,
                      channel_multiplier=K).then_inc(consts, 1)
            pool.memset(pads[:], 0.0).then_inc(pads_ready, 1)
            pool.wait_ge(pads_ready, 1)
            pool.iota(pads[:, :, ADDR].bitcast(I32), pattern=[[P, E + SPARE]], base=K * TOKENS,
                      channel_multiplier=1).then_inc(pads_ready, 1)

            def dispatch(h, lots):
                pool.wait_ge(slots_done, 2 * (h + 1))
                pool.wait_ge(gates_done, 2 * (h + 1))
                pool.wait_ge(rows_copied, 2 * (h + 1))
                for u, k in lots:
                    t = HT * h + u
                    pool.indirect_dma_start(
                        out=slots, out_offset=bass.IndirectOffsetOnAxis(ap=slot_of[:, k, t:t + 1], axis=0),
                        in_=rows[:, t, k, :], in_offset=None).then_inc(dispatched, 16)

            lots = [(u, k) for u in range(HT) for k in range(K)]
            one_over_std(0, 1)
            one_over_std(0, 2)
            pool.wait_ge(consts, 12)
            dispatch(0, lots[0:2])
            one_over_std(1, 0)
            dispatch(0, lots[2:7])
            one_over_std(1, 1)
            dispatch(0, lots[7:11])
            one_over_std(1, 2)
            dispatch(0, lots[11:])
            dispatch(1, lots)

            def send(i, j):
                pool.wait_ge(y_done, i + 1)
                pool.sem_inc(sends, 1)
                pool.indirect_dma_start(
                    out=returned,
                    out_offset=bass.IndirectOffsetOnAxis(ap=xg[j][:, ADDR:ADDR + 1].bitcast(I32), axis=0),
                    in_=y[j][:], in_offset=None).then_inc(y_sent[j], 16)

            with pool.Fori(0, BLOCKS // RING) as r:
                for j in range(RING):
                    send(r * RING + j, j)

            for s in range(SEQS):
                t = slice(CHUNKS * s, CHUNKS * (s + 1))
                pool.wait_ge(faggr_done, CHUNKS * (s + 1))
                pool.tensor_scalar(fve[:, t], fmv[:, t, 1], EPS, 1.0, ALU.add, ALU.mult).then_inc(feps_done, 1)
                pool.wait_ge(feps_done, s + 1)
                pool.tensor_tensor(out=frstd[:, t], in0=fve[:, t], in1=minus_half[:, 0:CHUNKS], op=ALU.pow) \
                    .then_inc(frstd_done, 1)

        @block.scalar
        def _(act):
            act.wait_ge(scalars_loaded, 16)
            act.activation(dtmp[:, 0:1], scalars[:, 1:2], ACT.Exp, scale=-1.0).then_inc(dexp_done, 1)
            act.dma_start(w1[:], w1_in.rearrange("e d f -> d e f")).then_inc(w1_loaded, 16)
            act.dma_start(w2[:], w2_in.rearrange("e (c f) d -> f e c d", f=P)).then_inc(w2_loaded, 16)
            act.wait_ge(mix_mm, 1)
            act.activation(mix[:], mix_ps, ACT.Copy, scale=scalars[:, 0:1]).then_inc(mix_done, 1)
            with act.Fori(0, HALVES) as h:
                for q in range(HS):
                    act.wait_ge(holo_mm, h * HS + (q + 1))
                    act.activation(holo_t[:, q, :], holo_ps[q][:], ACT.Copy).then_inc(holo_out, 1)
                act.wait_ge(n3_done, h * HT + HT)
                for q in range(HS):
                    act.wait_ge(n3t_mm, h * HS + (q + 1))
                    act.activation(n3_t[:, q, :], n3t_ps[q][:], ACT.Copy).then_inc(n3t_out, 1)
                act.wait_ge(lsub_done, h + 1)
                act.activation(ex[:], lg[:], ACT.Exp).then_inc(exp_done, 1)
                for k in range(K):
                    act.activation(rows[:, bass.ds(h * HT, HT), k, 0:D], n3[:], ACT.Copy).then_inc(rows_copied, 1)

            def block_work(i, j, first):
                act.wait_ge(up_mm, i + 1)
                if not first:
                    act.wait_ge(hidt_mm, i - 1)
                act.activation(hid[j % 2][:], up_ps[j % 2][:], ACT.Gelu_apprx_tanh).then_inc(gelu_done, 1)

            def rows_out(i, j, first):
                act.wait_ge(xgt_mm, i + 1)
                if not first:
                    act.wait_ge(up_mm, i - 1)
                act.activation(xg_t[j % 2][:], xgt_ps[j % 2][:, 0:P], ACT.Copy).then_inc(xgt_out, 1)

            rows_out(0, 0, True)
            rows_out(1, 1, True)
            for j in range(2):
                block_work(j, j, True)
                rows_out(j + 2, j, False)
            with act.Fori(1, BLOCKS // 2 - 1) as r:
                for j in range(2):
                    block_work(r * 2 + j, j, False)
                    rows_out(r * 2 + (j + 2), j, False)
            for j in range(2):
                block_work(BLOCKS - 2 + j, j, False)

        @block.tensor
        def _(pe):
            pe.wait_ge(keys_loaded, 32)
            pe.matmul(mix_ps, hankel[:, 0, :], hankel[:, 1, :], start=True, stop=True).then_inc(mix_mm, 1)
            pe.wait_ge(decay_m_done, 3)
            pe.wait_ge(mix_done, 1)
            pe.wait_ge(consts, 4)
            pe.wait_ge(router_loaded, 16)
            with pe.Fori(0, HALVES) as h:
                for q in range(HS):
                    pe.wait_ge(n1_done, h * HT + CHUNKS * (q + 1))
                    for c in range(CHUNKS):
                        mm = pe.matmul(holo_ps[q][:, P * c:SEQ], n1[:, CHUNKS * q + c, :],
                                       decay_m[:, 0:SEQ - P * c], start=c == 0, stop=c == CHUNKS - 1)
                    mm.then_inc(holo_mm, 1)
                for q in range(HS):
                    pe.wait_ge(holo_out, h * HS + (q + 1))
                    for c in range(CHUNKS):
                        mm = pe.matmul(ret_ps[q][:, P * c:P * (c + 1)], holo_t[:, q, P * c:P * (c + 1)], mix[:],
                                       start=True, stop=True)
                    mm.then_inc(ret_mm, 1)
                for q in range(HS):
                    pe.wait_ge(n3_done, h * HT + CHUNKS * (q + 1))
                    for c in range(CHUNKS):
                        mm = pe.transpose(n3t_ps[q][:, P * c:P * (c + 1)], n3[:, CHUNKS * q + c, :], ident[:])
                    mm.then_inc(n3t_mm, 1)
                for q in range(HS):
                    pe.wait_ge(n3t_out, h * HS + (q + 1))
                    for c in range(CHUNKS):
                        mm = pe.matmul(logit_ps[:, CHUNKS * q + c, :], n3_t[:, q, P * c:P * (c + 1)], router[:],
                                       start=True, stop=True)
                mm.then_inc(logits_mm, 1)
                pe.wait_ge(picks_done, h + 1)
                pe.matmul(rank_ps, below[:], picks[:], start=True, stop=False)
                for u in range(HT - 1):
                    later = HT - 1 - u
                    pe.matmul(rank_ps[:, u + 1:, :], ones[:],
                              picks[:, u:u + 1, :].broadcast_to([P, later, E]), start=False, stop=u == HT - 2)
                for u in range(HT):
                    mm = pe.matmul(total_ps, ones[:], picks[:, u, :], start=u == 0, stop=u == HT - 1)
                mm.then_inc(rank_mm, 1)

            def turn_rows(i, j, k, first):
                pe.wait_ge(xg_loaded[j], (i - j) * (16 // RING) + 16)
                if not first:
                    pe.wait_ge(xgt_out, i - 1)
                pe.transpose(xgt_ps[k % 2][:, 0:P], xg[j][:, 0:D], ident[:]).then_inc(xgt_mm, 1)

            def up(i, k, first):
                e = pe.value_load(block_expert[0:1, bass.ds(i, 1)], min_val=0, max_val=E - 1)
                pe.wait_ge(xgt_out, i + 1)
                if not first:
                    pe.wait_ge(gelu_done, i - 1)
                pe.matmul(up_ps[k % 2][:], xg_t[k % 2][:], w1[:, bass.ds(e, 1), :].rearrange("p a f -> p (a f)"),
                          start=True, stop=True).then_inc(up_mm, 1)

            def turn_hidden(i, k, first):
                pe.wait_ge(gelu_done, i + 1)
                if not first:
                    pe.wait_ge(hidt_out, i - 1)
                for c in range(FC):
                    mm = pe.transpose(hidt_ps[k % 2][:, P * c:P * (c + 1)], hid[k % 2][:, P * c:P * (c + 1)], ident[:])
                mm.then_inc(hidt_mm, 1)

            def down(i, k, first):
                e = pe.value_load(block_expert[0:1, bass.ds(i, 1)], min_val=0, max_val=E - 1)
                pe.wait_ge(hidt_out, i + 1)
                if not first:
                    pe.wait_ge(y_done, i - 1)
                for c in range(FC):
                    mm = pe.matmul(y_ps[k % 2][:, 0:D], hid_t[k % 2][:, c, :],
                                   w2[:, bass.ds(e, 1), c, :].rearrange("p a f -> p (a f)"),
                                   start=c == 0, stop=c == FC - 1)
                mm.then_inc(down_mm, 1)

            pe.wait_ge(table_done, 2)
            pe.wait_ge(w1_loaded, 16)
            pe.wait_ge(w2_loaded, 16)
            turn_rows(0, 0, 0, True)
            turn_rows(1, 1, 1, True)
            up(0, 0, True)
            for j in range(RING):
                turn_hidden(j, j, j < 2)
                up(j + 1, j + 1, j + 1 < 2)
                down(j, j, j < 2)
                turn_rows(j + 2, (j + 2) % RING, j, False)
            with pe.Fori(1, BLOCKS // RING - 1) as r:
                i = r * RING
                for j in range(RING):
                    turn_hidden(i + j, j, False)
                    up(i + (j + 1), j + 1, False)
                    down(i + j, j, False)
                    if j < 2:
                        turn_rows(i + (j + 2), j + 2, j, False)
                    else:
                        pe.wait_ge(xg_loaded[j - 2], (i * (16 // RING)) + 32)
                        pe.wait_ge(xgt_out, i + (j + 1))
                        pe.transpose(xgt_ps[j % 2][:, 0:P], xg[j - 2][:, 0:D], ident[:]).then_inc(xgt_mm, 1)
            last = BLOCKS - RING
            for j in range(RING):
                turn_hidden(last + j, j, False)
                if j + 1 < RING:
                    up(last + j + 1, j + 1, False)
                down(last + j, j, False)
                if j + 2 < RING:
                    turn_rows(last + j + 2, j + 2, j, False)

        @block.vector
        def _(dve):
            dve.wait_ge(dexp_done, 1)
            dve.tensor_scalar(dtmp[:, 1:2], dtmp[:, 0:1], 1.0, None, ALU.add).then_inc(sig, 1)
            dve.wait_ge(sig, 1)
            dve.reciprocal(dpow[:, 0:1], dtmp[:, 1:2]).then_inc(sig, 2)

            def statistics(h, n, src):
                for u in range(HT):
                    dve.bn_stats(st[:, u, :], src(u)).then_inc(stats_done[n], 1)
                dve.wait_ge(stats_done[n], h * HT + HT)
                dve.sem_inc(aggregations, 1)
                for u in range(HT):
                    dve.bn_aggr(mv[n][:, u, :], st[:, u, :]).then_inc(aggr_done[n], 1)

            dve.wait_ge(consts, 4)
            for b in range(8):
                dve.wait_ge(sig, 3)
                if b:
                    dve.wait_ge(dpow_done, b)
                    dve.wait_ge(toep_done, b)
                src, dst = toep[b % 2], toep[(b + 1) % 2]
                sh = 1 << b
                dve.scalar_tensor_tensor(out=dst[:, P:], in0=src[:, P - sh:P - sh + W2P], scalar=dpow[:, b:b + 1],
                                         in1=src[:, P:], op0=ALU.mult, op1=ALU.add).then_inc(toep_done, 1)
            dve.wait_ge(toep_done, 8)
            dve.tensor_copy(decay_m[:, 0:W2P], toep[0][:, P:]).then_inc(decay_m_done, 1)
            dve.wait_ge(dpow_done, 8)
            for c in range(2, CHUNKS):
                dve.tensor_scalar(decay_m[:, P * c:P * (c + 1)], toep[0][:, 2 * P:3 * P],
                                  dpow[:, 7 + (c - 2):8 + (c - 2)], None, ALU.mult).then_inc(decay_m_done, 1)

            dve.wait_ge(x_loaded, 16 * SEQS)
            with dve.Fori(0, HALVES) as h:
                statistics(h, 0, lambda u: x[:, bass.ds(h * HT + u, 1), :].rearrange("p a d -> p (a d)"))
                dve.wait_ge(rstd_done[0], h + 1)
                for u in range(HT):
                    dve.tensor_scalar(n1[:, u, :], x[:, bass.ds(h * HT + u, 1), :].rearrange("p a d -> p (a d)"),
                                      mv[0][:, u, 0:1], rstd[0][:, u:u + 1], ALU.subtract, ALU.mult) \
                        .then_inc(n1_done, 1)
                for q in range(HS):
                    dve.wait_ge(ret_mm, h * HS + (q + 1))
                    dve.tensor_tensor(out=mixed[:, CHUNKS * q:CHUNKS * (q + 1), :],
                                      in0=ret_ps[q][:].rearrange("p (c d) -> p c d", d=D),
                                      in1=n1[:, CHUNKS * q:CHUNKS * (q + 1), :], op=ALU.add).then_inc(mixed_done, 1)
                dve.wait_ge(mixed_done, h * HS + HS)
                statistics(h, 1, lambda u: mixed[:, u, :])
                dve.wait_ge(rstd_done[1], h + 1)
                for u in range(HT):
                    dve.tensor_scalar(normed[:, u, :], mixed[:, u, :], mv[1][:, u, 0:1], rstd[1][:, u:u + 1],
                                      ALU.subtract, ALU.mult).then_inc(normed_done, 1)
                dve.wait_ge(normed_done, h * HT + HT)
                dve.tensor_tensor(out=x1[:, bass.ds(h * HT, HT), :], in0=x[:, bass.ds(h * HT, HT), :],
                                  in1=normed[:], op=ALU.add).then_inc(x1_done, 1)
                dve.wait_ge(x_loaded, 16 * SEQS)
                dve.wait_ge(x1_done, h + 1)
                statistics(h, 2, lambda u: x1[:, bass.ds(h * HT + u, 1), :].rearrange("p a d -> p (a d)"))
                dve.wait_ge(rstd_done[2], h + 1)
                for u in range(HT):
                    dve.tensor_scalar(n3[:, u, :], x1[:, bass.ds(h * HT + u, 1), :].rearrange("p a d -> p (a d)"),
                                      mv[2][:, u, 0:1], rstd[2][:, u:u + 1], ALU.subtract, ALU.mult) \
                        .then_inc(n3_done, 1)

                STEPS = 17
                done = [0]

                def step(instruction):
                    done[0] += 1
                    instruction.then_inc(router_step, 1)
                    dve.wait_ge(router_step, h * STEPS + done[0])

                def wide(v):
                    return v.unsqueeze(2).broadcast_to([P, HT, E])

                dve.wait_ge(logits_mm, h + 1)
                step(dve.tensor_reduce(out=lmax[:], in_=logit_ps, axis=AX.X, op=ALU.max))
                dve.tensor_tensor(out=lg[:], in0=logit_ps, in1=wide(lmax[:]), op=ALU.subtract).then_inc(lsub_done, 1)
                dve.wait_ge(exp_done, h + 1)
                step(dve.tensor_reduce(out=esum[:], in_=ex[:], axis=AX.X, op=ALU.add))
                step(dve.reciprocal(einv[:], esum[:]))
                step(dve.tensor_tensor(out=prob[:], in0=ex[:], in1=wide(einv[:]), op=ALU.mult))
                for k, src in ((0, prob), (1, rest)):
                    step(dve.tensor_reduce(out=top[k][:], in_=src[:], axis=AX.X, op=ALU.max))
                    step(dve.tensor_tensor(out=tied[:], in0=src[:], in1=wide(top[k][:]), op=ALU.is_equal))
                    step(dve.tensor_tensor(out=ranked[:], in0=tied[:], in1=prefer[:], op=ALU.mult))
                    step(dve.tensor_reduce(out=best[:], in_=ranked[:], axis=AX.X, op=ALU.max))
                    step(dve.tensor_tensor(out=pick[k][:], in0=ranked[:], in1=wide(best[:]), op=ALU.is_equal))
                    if k == 0:
                        step(dve.scalar_tensor_tensor(out=rest[:], in0=pick[0][:], scalar=-2.0, in1=prob[:],
                                                      op0=ALU.mult, op1=ALU.add))
                dve.tensor_tensor(out=picks[:], in0=pick[0][:], in1=pick[1][:], op=ALU.add).then_inc(picks_done, 1)
                for k in range(K):
                    dve.tensor_copy(rows[:, bass.ds(h * HT, HT), k, GATE], top[k][:]).then_inc(gates_done, 1)
                step(dve.tensor_tensor(out=base[:], in0=count[:], in1=region_row[:], op=ALU.add))
                dve.wait_ge(rank_mm, h + 1)
                step(dve.tensor_tensor(out=place[:], in0=rank_ps,
                                       in1=base[:].unsqueeze(1).broadcast_to([P, HT, E]), op=ALU.add))
                dve.tensor_tensor(out=count[:], in0=count[:], in1=total_ps, op=ALU.add).then_inc(table_step, 1)
                for k in range(K):
                    dve.tensor_tensor(out=(chosen if k == 0 else ranked)[:], in0=pick[k][:], in1=place[:],
                                      op=ALU.mult).then_inc(chosen_done, 1)
                dve.wait_ge(chosen_done, h * 2 + 2)
                dve.tensor_reduce(out=slotf[:], in_=chosen[:], axis=AX.X, op=ALU.add).then_inc(slotf_done, 1)
                dve.tensor_reduce(out=best[:], in_=ranked[:], axis=AX.X, op=ALU.add).then_inc(slotf_done, 1)
                dve.wait_ge(slotf_done, h * 2 + 2)
                for k, src in ((0, slotf), (1, best)):
                    dve.tensor_copy(slot_of[:, k, bass.ds(h * HT, HT)], src[:]).then_inc(slots_done, 1)
                assert done[0] == STEPS, done
                dve.wait_ge(rows_copied, h * K + K)

            tstep = [HALVES]

            def table(instruction):
                tstep[0] += 1
                instruction.then_inc(table_step, 1)
                dve.wait_ge(table_step, tstep[0])

            dve.wait_ge(table_step, HALVES)
            dve.tensor_tensor(out=pad_row[:], in0=count[:], in1=region_row[:], op=ALU.add).then_inc(pad_rows_done, 1)
            table(dve.tensor_scalar(cnt_i[:], count[:], float(P - 1), None, ALU.add))
            table(dve.tensor_single_scalar(nblk_i[:], cnt_i[:], 7, ALU.arith_shift_right))
            table(dve.tensor_copy(nblk[:], nblk_i[:]))
            table(dve.tensor_copy(cum[0][:, 4:], nblk[:]))
            for b in range(3):
                src, dst, sh = cum[b % 2], cum[(b + 1) % 2], 1 << b
                table(dve.tensor_tensor(out=dst[:, 4:], in0=src[:, 4:], in1=src[:, 4 - sh:4 - sh + E], op=ALU.add))
            full = [P, BLOCKS, E]
            table(dve.tensor_tensor(out=past[:], in0=cum[1][:, 4:].unsqueeze(1).broadcast_to(full),
                                    in1=step_no[:].unsqueeze(2).broadcast_to(full), op=ALU.is_le))
            table(dve.tensor_reduce(out=be[:], in_=past[:], axis=AX.X, op=ALU.add))
            dve.tensor_scalar(block_expert[:], be[:], float(E - 1), None, ALU.min).then_inc(table_done, 1)
            table(dve.tensor_tensor(out=pastn[:], in0=past[:], in1=nblk[:].unsqueeze(1).broadcast_to(full),
                                    op=ALU.mult))
            table(dve.tensor_reduce(out=bn[:], in_=pastn[:], axis=AX.X, op=ALU.add))
            table(dve.tensor_tensor(out=bt[:], in0=step_no[:], in1=bn[:], op=ALU.subtract))
            table(dve.tensor_scalar(bt[:], bt[:], float(P), None, ALU.mult))
            dve.scalar_tensor_tensor(out=block_row[:], in0=be[:], scalar=float(REGION), in1=bt[:],
                                     op0=ALU.mult, op1=ALU.add).then_inc(table_done, 1)

            def turned(i, k, first):
                dve.wait_ge(hidt_mm, i + 1)
                if not first:
                    dve.wait_ge(down_mm, i - 1)
                dve.tensor_copy(hid_t[k % 2][:].rearrange("p c t -> p (c t)"), hidt_ps[k % 2][:]) \
                    .then_inc(hidt_out, 1)

            def gated(i, j, first):
                dve.wait_ge(down_mm, i + 1)
                if not first:
                    dve.wait_ge(y_sent[j], (i - j) * (16 // RING))
                dve.tensor_scalar(y[j][:], y_ps[j % 2][:, 0:D], xg[j][:, GATE:GATE + 1], None, ALU.mult) \
                    .then_inc(y_done, 1)

            for j in range(RING):
                turned(j, j, j < 2)
                gated(j, j, True)
            with dve.Fori(1, BLOCKS // RING) as r:
                for j in range(RING):
                    turned(r * RING + j, j, False)
                    gated(r * RING + j, j, False)

            for s in range(SEQS):
                t = slice(CHUNKS * s, CHUNKS * (s + 1))
                dve.wait_ge(yk_loaded[s], 16)
                dve.tensor_tensor(out=ff[:, t, :], in0=yk[:, t, 0:D], in1=yk[:, t, D:2 * D], op=ALU.add) \
                    .then_inc(ff_done, 1)
                dve.wait_ge(ff_done, s + 1)
                for u in range(CHUNKS * s, CHUNKS * (s + 1)):
                    dve.bn_stats(fst[:, u, :], ff[:, u, :]).then_inc(fstats_done, 1)
                dve.wait_ge(fstats_done, CHUNKS * (s + 1))
                for u in range(CHUNKS * s, CHUNKS * (s + 1)):
                    dve.bn_aggr(fmv[:, u, :], fst[:, u, :]).then_inc(faggr_done, 1)
            for s in range(SEQS):
                t = slice(CHUNKS * s, CHUNKS * (s + 1))
                dve.wait_ge(frstd_done, s + 1)
                for u in range(CHUNKS * s, CHUNKS * (s + 1)):
                    dve.tensor_scalar(fn[:, u, :], ff[:, u, :], fmv[:, u, 0:1], frstd[:, u:u + 1],
                                      ALU.subtract, ALU.mult).then_inc(fn_done, 1)
                dve.wait_ge(fn_done, CHUNKS * (s + 1))
                dve.tensor_tensor(out=fo[:, t, :], in0=fn[:, t, :], in1=x1[:, t, :], op=ALU.add).then_inc(fo_done, 1)


def kernel(**inputs):
    import numpy as np
    import concourse.bacc as bacc
    from concourse.bass_utils import run_bass_kernel_spmd

    a = {n: np.asarray(v) for n, v in inputs.items()}
    back = (-np.arange(2 * P)) % P
    arrays = {
        "x_dram": np.ascontiguousarray(a["L0_attn_x"]),
        "keys_dram": np.stack([a["L0_attn_bind_key"][back], a["L0_attn_unbind_key"][back]]),
        "scalars_dram": np.ascontiguousarray(np.broadcast_to(
            np.concatenate([a["L0_attn_gate"].reshape(1), a["L0_attn_decay"].reshape(1)]), (P, 2))),
        "router_dram": np.ascontiguousarray(a["L0_ffn_router_w"]),
        "w1_dram": np.ascontiguousarray(a["L0_ffn_w1"]),
        "w2_dram": np.ascontiguousarray(a["L0_ffn_w2"]),
    }
    nc = bacc.Bacc("TRN2", target_bir_lowering=False, num_devices=1)
    aps = [nc.dram_tensor(n, v.shape, F32, kind="ExternalInput").ap() for n, v in arrays.items()]
    out = nc.dram_tensor("out_dram", (SEQS, SEQ, D), F32, kind="ExternalOutput").ap()
    slots = nc.dram_tensor("slots_dram", [E * REGION + SPARE * P, ROW], F32, kind="Internal").ap()
    returned = nc.dram_tensor("returned_dram", [K * TOKENS + (E + SPARE) * P, D], F32, kind="Internal").ap()
    build(nc, *aps, out, slots, returned)
    r = run_bass_kernel_spmd(nc, [arrays], core_ids=[0])
    return r.results[0]["out_dram"]
```

```python
from contextlib import ExitStack

import concourse.bass as bass
from concourse import mybir

P = 128
D = 128
SEQS, SEQ = 4, 512
TOKENS = SEQS * SEQ
TILES = TOKENS // P
CHUNKS = SEQ // P
E, F, K = 8, 512, 2
FC = F // P
EPS = 1e-5
LOWEST = -3e38

REGION = TOKENS + P
FULL_BLOCKS = K * TOKENS // P
BLOCKS = (K * TOKENS + E * (P - 1)) // P
SPARE = BLOCKS - FULL_BLOCKS
ROW = D + 2
ADDR, GATE = D, D + 1
RING = 8
ROUNDS = BLOCKS // RING
REST = BLOCKS - ROUNDS * RING

F32 = mybir.dt.float32
I32 = mybir.dt.int32
BF16 = mybir.dt.bfloat16
ALU = mybir.AluOpType
ACT = mybir.ActivationFunctionType
AX = mybir.AxisListType


def build(nc, x_in, keys_in, scalars_in, router_in, w1_in, w2_in, out, slots, returned):
    ctx = ExitStack()
    with ctx:
        def sb(name, shape, dt=F32):
            return ctx.enter_context(nc.sbuf_tensor(name, shape, dt))

        def sem(name):
            return ctx.enter_context(nc.semaphore(name))

        x = sb("x", [P, TILES, D])
        n1 = sb("n1", [P, TILES, D])
        mixed = sb("mixed", [P, TILES, D])
        normed = sb("normed", [P, TILES, D])
        x1 = sb("x1", [P, TILES, D])
        n3 = sb("n3", [P, TILES, D])
        holo_t = sb("holo_t", [P, SEQS, SEQ])
        n3_t = sb("n3_t", [P, SEQS, SEQ])
        rows = sb("rows", [P, TILES, K, ROW])
        slot_of = sb("slot_of", [P, TILES, K], I32)
        w1 = sb("w1", [P, E, F])
        w2 = sb("w2", [P, E, FC, D])
        router = sb("router", [P, E])
        ident = sb("ident", [P, P])
        below = sb("below", [P, P], BF16)
        ones = sb("ones", [P, P], BF16)
        minus_half = sb("minus_half", [P, CHUNKS])
        prefer = sb("prefer", [P, CHUNKS, E])
        region_row = sb("region_row", [P, E])
        step_no = sb("step_no", [P, BLOCKS])
        pads = sb("pads", [P, E + SPARE, ROW])
        scalars = sb("scalars", [P, 2])
        hankel = sb("hankel", [P, 2, P])
        mix = sb("mix", [P, P])
        dpow = sb("dpow", [P, 9])
        dtmp = sb("dtmp", [P, 2])
        toep = [sb(f"toep{i}", [P, 3 * P]) for i in range(2)]
        decay_m = sb("decay_m", [P, SEQ])
        st = [sb(f"st{n}", [P, TILES, 6]) for n in range(4)]
        mv = [sb(f"mv{n}", [P, TILES, 2]) for n in range(4)]
        ve = [sb(f"ve{n}", [P, TILES]) for n in range(4)]
        rstd = [sb(f"rstd{n}", [P, TILES]) for n in range(4)]
        neg_mean = [sb(f"neg_mean{n}", [P, TILES]) for n in range(4)]
        shift = [sb(f"shift{n}", [P, TILES]) for n in range(4)]
        lg = sb("lg", [P, CHUNKS, E])
        lmax = sb("lmax", [P, CHUNKS])
        second = sb("second", [P, CHUNKS])
        ldif = sb("ldif", [P, CHUNKS, E + 1])
        ex = sb("ex", [P, CHUNKS, E + 1])
        esum = sb("esum", [P, CHUNKS])
        einv = sb("einv", [P, CHUNKS])
        rest = sb("rest", [P, CHUNKS, E])
        tied = sb("tied", [P, CHUNKS, E])
        ranked = [sb(f"ranked{k}", [P, CHUNKS, E]) for k in range(K)]
        best = [sb(f"best{k}", [P, CHUNKS]) for k in range(K)]
        pick = sb("pick", [P, CHUNKS, K, E])
        picks = sb("picks", [P, SEQS, CHUNKS, E], BF16)
        count = sb("count", [P, E])
        base = sb("base", [P, E])
        place = sb("place", [P, CHUNKS, E])
        chosen = sb("chosen", [P, CHUNKS, K, E])
        slotf = sb("slotf", [P, CHUNKS, K])
        pad_row = sb("pad_row", [P, E], I32)
        cnt_i = sb("cnt_i", [P, E], I32)
        nblk_i = sb("nblk_i", [P, E], I32)
        nblk = sb("nblk", [P, E])
        cum = [sb(f"cum{i}", [P, 4 + E]) for i in range(2)]
        past = sb("past", [P, BLOCKS, E])
        pastn = sb("pastn", [P, BLOCKS, E])
        be = sb("be", [P, BLOCKS])
        bn = sb("bn", [P, BLOCKS])
        bt = sb("bt", [P, BLOCKS])
        block_expert = sb("block_expert", [P, BLOCKS], I32)
        block_row = sb("block_row", [P, BLOCKS], I32)
        xg = [sb(f"xg{i}", [P, ROW]) for i in range(RING)]
        xg_t = [sb(f"xg_t{i}", [P, P]) for i in range(2)]
        w1_now = [sb(f"w1_now{i}", [P, F]) for i in range(2)]
        hid_t = [sb(f"hid_t{i}", [P, FC, P]) for i in range(2)]
        y = [sb(f"y{i}", [P, D]) for i in range(RING)]
        warm = sb("warm", [P, 1])
        yk = sb("yk", [P, TILES, K * D])

        bank = [ctx.enter_context(nc.psum_tensor(f"bank{i}", [P, 512], F32)) for i in range(8)]
        holo_ps, ret_ps, n3t_ps = bank[0:2], bank[2:4], bank[4:6]
        logit_ps = bank[6][:, 0:CHUNKS * E].rearrange("p (u e) -> p u e", e=E)
        mix_ps = bank[7][:, 0:P]
        rank_ps = bank[7][:, 0:CHUNKS * E].rearrange("p (u e) -> p u e", e=E)
        total_ps = bank[7][:, CHUNKS * E:CHUNKS * E + E]
        xgt_ps, up_ps, y_ps = bank[0:2], bank[2:4], bank[6:8]

        scalars_loaded = sem("scalars_loaded")
        keys_loaded = sem("keys_loaded")
        x_loaded = [sem(f"x_loaded{i}") for i in range(SEQS)]
        router_loaded = sem("router_loaded")
        w1_loaded = sem("w1_loaded")
        w2_loaded = sem("w2_loaded")
        zeroed = sem("zeroed")
        toep_start = sem("toep_start")
        ident_done = sem("ident_done")
        half_done = sem("half_done")
        router_consts = sem("router_consts")
        table_consts = sem("table_consts")
        sig = sem("sig")
        dexp_done = sem("dexp_done")
        dpow_done = sem("dpow_done")
        toep_done = sem("toep_done")
        decay_m_done = sem("decay_m_done")
        mix_mm = sem("mix_mm")
        mix_done = sem("mix_done")
        stats_done = [sem(f"stats_done{i}") for i in range(4)]
        aggr_done = [sem(f"aggr_done{i}") for i in range(4)]
        eps_added = [sem(f"eps_added{i}") for i in range(4)]
        rstd_done = [sem(f"rstd_done{i}") for i in range(4)]
        shift_done = [sem(f"shift_done{i}") for i in range(4)]
        n1_done = sem("n1_done")
        holo_mm = sem("holo_mm")
        holo_out = sem("holo_out")
        ret_mm = sem("ret_mm")
        mixed_done = sem("mixed_done")
        normed_done = sem("normed_done")
        x1_done = sem("x1_done")
        n3_done = sem("n3_done")
        n3t_mm = sem("n3t_mm")
        n3t_out = sem("n3t_out")
        rows_copied = sem("rows_copied")
        logits_mm = sem("logits_mm")
        logits_out = sem("logits_out")
        ldif_done = sem("ldif_done")
        exp_done = sem("exp_done")
        picks_done = sem("picks_done")
        rank_mm = sem("rank_mm")
        router_step = sem("router_step")
        slots_done = sem("slots_done")
        gates_done = sem("gates_done")
        dispatched = sem("dispatched")
        pads_ready = sem("pads_ready")
        spare_padded = sem("spare_padded")
        padded = sem("padded")
        pad_rows_done = sem("pad_rows_done")
        table_step = sem("table_step")
        table_done = sem("table_done")
        xg_loaded = [sem(f"xg_loaded{i}") for i in range(RING)]
        xgt_mm = sem("xgt_mm")
        xgt_out = sem("xgt_out")
        w1_ready = sem("w1_ready")
        up_mm = sem("up_mm")
        gelu_done = sem("gelu_done")
        down_mm = sem("down_mm")
        y_done = sem("y_done")
        sends = sem("sends")
        y_sent = [sem(f"y_sent{i}") for i in range(RING)]
        yk_loaded = [sem(f"yk_loaded{i}") for i in range(SEQS)]
        ff_done = sem("ff_done")
        fn_done = sem("fn_done")
        fo_done = sem("fo_done")
        stored = sem("stored")

        block = ctx.enter_context(nc.Block())
        x_tiles = x_in.rearrange("s (c p) d -> s p c d", p=P)
        out_tiles = out.rearrange("s (c p) d -> s p c d", p=P)

        def of_seq(s):
            return slice(CHUNKS * s, CHUNKS * (s + 1))

        def tiles_of(s):
            return range(CHUNKS * s, CHUNKS * (s + 1))

        PAIR = 2

        @block.sync
        def _(sp):
            sp.dma_start(scalars[:], scalars_in).then_inc(scalars_loaded, 16)
            for s in range(SEQS):
                sp.dma_start(x[:, of_seq(s), :], x_tiles[s]).then_inc(x_loaded[s], 16)
            sp.dma_start(router[:], router_in).then_inc(router_loaded, 16)
            sp.wait_ge(pads_ready, 2)
            sp.dma_start(slots[E * REGION:E * REGION + SPARE * P, :].rearrange("(b p) c -> p b c", p=P),
                         pads[:, E:, :]).then_inc(spare_padded, 16)
            sp.wait_ge(pad_rows_done, 1)
            for e in range(E):
                first = sp.value_load(pad_row[0:1, e:e + 1], min_val=0, max_val=E * REGION - P)
                sp.dma_start(slots[bass.ds(first, P), :], pads[:, e, :]).then_inc(padded, 16)
            sp.wait_ge(table_done, 2)
            sp.wait_ge(spare_padded, 16)
            sp.wait_ge(padded, 16 * E)
            sp.wait_ge(dispatched, 16 * TILES * K)

            def load_block(r, j):
                i = j if r is None else r * RING + j
                row = sp.value_load(block_row[0:1, bass.ds(i, 1)], min_val=0,
                                    max_val=E * REGION + (SPARE - 1) * P)
                if r is not None:
                    sp.wait_ge(y_sent[j], r * 16)
                sp.dma_start(xg[j][:], slots[bass.ds(row, P), :]).then_inc(xg_loaded[j], 16)

            for j in range(RING):
                load_block(None, j)
            with sp.Fori(1, ROUNDS) as r:
                for j in range(RING):
                    load_block(r, j)
            for j in range(REST):
                load_block(ROUNDS, j)
            for j in range(RING):
                sp.wait_ge(y_sent[j], 16 * (ROUNDS + (j < REST)))
            back = returned[0:K * TOKENS, :].rearrange("(s c p k) d -> s p c (k d)", c=CHUNKS, p=P, k=K)
            for s in range(SEQS):
                sp.dma_start(yk[:, of_seq(s), :], back[s]).then_inc(yk_loaded[s], 16)
            for s in range(SEQS):
                sp.wait_ge(fo_done, s + 1)
                sp.dma_start(out_tiles[s], normed[:, of_seq(s), :]).then_inc(stored, 16)
            sp.wait_ge(stored, 16 * SEQS)

        @block.gpsimd
        def _(pool):
            pool.memset(toep[0][:], 0.0).then_inc(zeroed, 1)
            pool.wait_ge(zeroed, 1)
            pool.affine_select(out=toep[0][:, P:], in_=toep[0][:, P:], compare_op=ALU.not_equal, fill=1.0, base=0,
                               pattern=[[-1, 2 * P]], channel_multiplier=1).then_inc(toep_start, 1)
            pool.memset(toep[1][:, 0:P], 0.0).then_inc(toep_start, 1)

            pool.wait_ge(sig, 3)
            for b in range(8):
                if b:
                    pool.wait_ge(dpow_done, b)
                pool.tensor_tensor(out=dpow[:, b + 1:b + 2], in0=dpow[:, b:b + 1], in1=dpow[:, b:b + 1],
                                   op=ALU.mult).then_inc(dpow_done, 1)
            pool.memset(minus_half[:], -0.5).then_inc(half_done, 1)
            pool.memset(ident[:], 0.0).then_inc(ident_done, 1)
            pool.wait_ge(ident_done, 1)
            pool.affine_select(out=ident[:], in_=ident[:], compare_op=ALU.not_equal, fill=1.0, base=0,
                               pattern=[[-1, P]], channel_multiplier=1).then_inc(ident_done, 1)
            pool.wait_ge(half_done, 1)

            def one_over_std(s, n, with_shift):
                t = of_seq(s)
                pool.wait_ge(aggr_done[n], CHUNKS * (s + 1))
                pool.tensor_scalar(ve[n][:, t], mv[n][:, t, 1], EPS, 1.0, ALU.add, ALU.mult).then_inc(eps_added[n], 1)
                if with_shift:
                    pool.tensor_scalar(neg_mean[n][:, t], mv[n][:, t, 0], -1.0, 0.0, ALU.mult, ALU.add) \
                        .then_inc(eps_added[n], 1)
                pool.wait_ge(eps_added[n], (s + 1) * (1 + with_shift))
                pool.tensor_tensor(out=rstd[n][:, t], in0=ve[n][:, t], in1=minus_half[:], op=ALU.pow) \
                    .then_inc(rstd_done[n], 1)
                if with_shift:
                    pool.wait_ge(rstd_done[n], s + 1)
                    pool.tensor_tensor(out=shift[n][:, t], in0=neg_mean[n][:, t], in1=rstd[n][:, t], op=ALU.mult) \
                        .then_inc(shift_done[n], 1)

            def dispatch(s, lots):
                pool.wait_ge(slots_done, s + 1)
                pool.wait_ge(gates_done, K * (s + 1))
                pool.wait_ge(rows_copied, K * (s + 1))
                for c, k in lots:
                    t = CHUNKS * s + c
                    pool.indirect_dma_start(
                        out=slots, out_offset=bass.IndirectOffsetOnAxis(ap=slot_of[:, t, k:k + 1], axis=0),
                        in_=rows[:, t, k, :], in_offset=None).then_inc(dispatched, 16)

            lots = [(c, k) for c in range(CHUNKS) for k in range(K)]
            for s in range(SEQS):
                one_over_std(s, 0, True)
            pool.memset(below[:], 1.0).then_inc(router_consts, 1)
            pool.memset(ones[:], 1.0).then_inc(router_consts, 1)
            pool.wait_ge(router_consts, 2)
            pool.affine_select(out=below[:], in_=below[:], compare_op=ALU.is_gt, fill=0.0, base=0,
                               pattern=[[1, P]], channel_multiplier=-1).then_inc(router_consts, 1)
            pool.iota(prefer[:], pattern=[[0, CHUNKS], [-1, E]], base=E, channel_multiplier=0,
                      allow_small_or_imprecise_dtypes=True).then_inc(router_consts, 1)
            pool.iota(region_row[:], pattern=[[REGION, E]], base=0, channel_multiplier=0,
                      allow_small_or_imprecise_dtypes=True).then_inc(router_consts, 1)
            pool.memset(count[:], 0.0).then_inc(router_consts, 1)
            pool.iota(rows[:, :, :, ADDR].bitcast(I32), pattern=[[K * P, TILES], [1, K]], base=0,
                      channel_multiplier=K).then_inc(router_consts, 1)
            one_over_std(0, 1, False)
            pool.memset(pads[:], 0.0).then_inc(pads_ready, 1)
            pool.wait_ge(pads_ready, 1)
            pool.iota(pads[:, :, ADDR].bitcast(I32), pattern=[[P, E + SPARE]], base=K * TOKENS,
                      channel_multiplier=1).then_inc(pads_ready, 1)
            one_over_std(1, 1, False)
            pool.iota(step_no[:], pattern=[[1, BLOCKS]], base=0, channel_multiplier=0,
                      allow_small_or_imprecise_dtypes=True).then_inc(table_consts, 1)
            for c in range(2):
                pool.memset(cum[c][:], 0.0).then_inc(table_consts, 1)
            pool.wait_ge(router_consts, 7)
            one_over_std(0, 2, True)
            one_over_std(2, 1, False)
            one_over_std(1, 2, True)
            one_over_std(3, 1, False)
            one_over_std(2, 2, True)
            dispatch(0, lots[:3])
            one_over_std(3, 2, True)
            dispatch(0, lots[3:])
            for s in range(1, SEQS):
                dispatch(s, lots)

            def send(i, j):
                pool.wait_ge(y_done, i + 1 + PAIR)
                pool.sem_inc(sends, 1)
                pool.indirect_dma_start(
                    out=returned,
                    out_offset=bass.IndirectOffsetOnAxis(ap=xg[j][:, ADDR:ADDR + 1].bitcast(I32), axis=0),
                    in_=y[j][:], in_offset=None).then_inc(y_sent[j], 16)

            with pool.Fori(0, ROUNDS) as r:
                for j in range(RING):
                    send(r * RING + j, j)
            for j in range(REST):
                send(ROUNDS * RING + j, j)
            for s in range(SEQS):
                one_over_std(s, 3, True)

        @block.scalar
        def _(act):
            for k in range(2):
                act.dma_start(hankel[:, k, :], bass.AP(keys_in.tensor, 2 * P * k, [[1, P], [1, P]])) \
                    .then_inc(keys_loaded, 16)
            act.wait_ge(scalars_loaded, 16)
            act.activation(dtmp[:, 0:1], scalars[:, 1:2], ACT.Exp, scale=-1.0).then_inc(dexp_done, 1)
            act.wait_ge(mix_mm, 1)
            act.activation(mix[:], mix_ps, ACT.Copy, scale=scalars[:, 0:1]).then_inc(mix_done, 1)

            def normalise(s, n, dst, src, done):
                act.wait_ge(shift_done[n], s + 1)
                for t in tiles_of(s):
                    act.activation(dst[:, t, :], src[:, t, :], ACT.Identity, bias=shift[n][:, t:t + 1],
                                   scale=rstd[n][:, t:t + 1]).then_inc(done, 1)

            def holo_copy(s):
                act.wait_ge(holo_mm, s + 1)
                act.activation(holo_t[:, s, :], holo_ps[s % 2][:], ACT.Copy).then_inc(holo_out, 1)

            def n3t_copy(s):
                act.wait_ge(n3t_mm, s + 1)
                act.activation(n3_t[:, s, :], n3t_ps[s % 2][:], ACT.Copy).then_inc(n3t_out, 1)

            def rows_copy(s):
                act.wait_ge(n3_done, CHUNKS * (s + 1))
                for k in range(K):
                    act.activation(rows[:, of_seq(s), k, 0:D], n3[:, of_seq(s), :], ACT.Copy).then_inc(rows_copied, 1)

            def exps(s):
                act.wait_ge(ldif_done, 2 * (s + 1))
                act.activation(ex[:], ldif[:], ACT.Exp).then_inc(exp_done, 1)

            act.wait_ge(decay_m_done, 1)
            act.wait_ge(dpow_done, 8)
            for c in range(2, CHUNKS):
                act.activation(decay_m[:, P * c:P * (c + 1)], decay_m[:, P:2 * P], ACT.Copy,
                               scale=dpow[:, 5 + c:6 + c]).then_inc(decay_m_done, 1)
            normalise(0, 0, n1, x, n1_done)
            normalise(1, 0, n1, x, n1_done)
            holo_copy(0)
            normalise(2, 0, n1, x, n1_done)
            holo_copy(1)
            normalise(3, 0, n1, x, n1_done)
            holo_copy(2)
            holo_copy(3)
            act.dma_start(w1[:], w1_in.rearrange("e d f -> d e f")).then_inc(w1_loaded, 16)
            act.dma_start(w2[:], w2_in.rearrange("e (c f) d -> f e c d", f=P)).then_inc(w2_loaded, 16)
            for s in range(SEQS):
                normalise(s, 2, n3, x1, n3_done)
                n3t_copy(s)
                rows_copy(s)
                exps(s)

            act.sem_inc(xgt_out, PAIR)
            act.sem_inc(gelu_done, PAIR)
            act.activation(warm[:], scalars[:, 0:1], ACT.Gelu_apprx_tanh)

            def rows_out(i, k):
                act.wait_ge(xgt_mm, i + 1)
                act.wait_ge(up_mm, i + 1)
                act.activation(xg_t[k % 2][:], xgt_ps[k % 2][:, 0:P], ACT.Copy).then_inc(xgt_out, 1)

            def gelu(i, k):
                act.wait_ge(up_mm, i + 1 + PAIR)
                act.wait_ge(down_mm, i + 1)
                act.activation(hid_t[k % 2][:].rearrange("p c t -> p (c t)"), up_ps[k % 2][:],
                               ACT.Gelu_apprx_tanh).then_inc(gelu_done, 1)

            rows_out(0, 0)
            rows_out(1, 1)
            with act.Fori(0, ROUNDS) as r:
                for j in range(RING):
                    gelu(r * RING + j, j)
                    rows_out(r * RING + (j + 2), j)
            for j in range(REST):
                gelu(ROUNDS * RING + j, j)
                if j + 2 < REST:
                    rows_out(ROUNDS * RING + j + 2, j)
            for s in range(SEQS):
                normalise(s, 3, mixed, n1, fn_done)

        @block.tensor
        def _(pe):
            pe.wait_ge(keys_loaded, 32)
            pe.matmul(mix_ps, hankel[:, 0, :], hankel[:, 1, :], start=True, stop=True).then_inc(mix_mm, 1)
            pe.wait_ge(decay_m_done, CHUNKS - 1)

            def hologram(s):
                pe.wait_ge(n1_done, CHUNKS * (s + 1))
                if s >= 2:
                    pe.wait_ge(holo_out, s - 1)
                for c in range(CHUNKS):
                    mm = pe.matmul(holo_ps[s % 2][:, P * c:SEQ], n1[:, CHUNKS * s + c, :],
                                   decay_m[:, 0:SEQ - P * c], start=c == 0, stop=c == CHUNKS - 1)
                mm.then_inc(holo_mm, 1)

            def retrieve(s):
                pe.wait_ge(holo_out, s + 1)
                if s >= 2:
                    pe.wait_ge(mixed_done, s - 1)
                for c in range(CHUNKS):
                    mm = pe.matmul(ret_ps[s % 2][:, P * c:P * (c + 1)], holo_t[:, s, P * c:P * (c + 1)], mix[:],
                                   start=True, stop=True)
                mm.then_inc(ret_mm, 1)

            def logits(s):
                pe.wait_ge(n3_done, CHUNKS * (s + 1))
                for c in range(CHUNKS):
                    mm = pe.transpose(n3t_ps[s % 2][:, P * c:P * (c + 1)], n3[:, CHUNKS * s + c, :], ident[:])
                mm.then_inc(n3t_mm, 1)
                pe.wait_ge(n3t_out, s + 1)
                if s:
                    pe.wait_ge(logits_out, s)
                for c in range(CHUNKS):
                    mm = pe.matmul(logit_ps[:, c, :], n3_t[:, s, P * c:P * (c + 1)], router[:],
                                   start=True, stop=True)
                mm.then_inc(logits_mm, 1)

            def ranks(s):
                pe.wait_ge(picks_done, s + 1)
                pe.matmul(rank_ps, below[:], picks[:, s, :, :], start=True, stop=False)
                for c in range(CHUNKS - 1):
                    pe.matmul(rank_ps[:, c + 1:, :], ones[:],
                              picks[:, s, c:c + 1, :].broadcast_to([P, CHUNKS - 1 - c, E]),
                              start=False, stop=c == CHUNKS - 2)
                for c in range(CHUNKS):
                    mm = pe.matmul(total_ps, ones[:], picks[:, s, c, :], start=c == 0, stop=c == CHUNKS - 1)
                mm.then_inc(rank_mm, 1)

            pe.wait_ge(mix_done, 1)
            hologram(0)
            hologram(1)
            retrieve(0)
            hologram(2)
            retrieve(1)
            hologram(3)
            retrieve(2)
            retrieve(3)
            pe.wait_ge(ident_done, 2)
            pe.wait_ge(router_loaded, 16)
            pe.wait_ge(router_consts, 7)
            logits(0)
            for s in range(SEQS):
                ranks(s)
                if s + 1 < SEQS:
                    logits(s + 1)

            def turn_rows(i, r, j, k):
                pe.wait_ge(xg_loaded[j], r * 16 + 16)
                pe.wait_ge(xgt_out, i + 1)
                pe.transpose(xgt_ps[k % 2][:, 0:P], xg[j][:, 0:D], ident[:]).then_inc(xgt_mm, 1)

            def up(i, k):
                pe.wait_ge(w1_ready, i + 1 + PAIR)
                pe.wait_ge(xgt_out, i + 1 + PAIR)
                pe.wait_ge(gelu_done, i + 1)
                for c in range(FC):
                    mm = pe.matmul(up_ps[k % 2][:, P * c:P * (c + 1)], w1_now[k % 2][:, P * c:P * (c + 1)],
                                   xg_t[k % 2][:], start=True, stop=True)
                mm.then_inc(up_mm, 1)

            def down(i, k):
                e = pe.value_load(block_expert[0:1, bass.ds(i, 1)], min_val=0, max_val=E - 1)
                pe.wait_ge(gelu_done, i + 1 + PAIR)
                pe.wait_ge(y_done, i + 1)
                for c in range(FC):
                    mm = pe.matmul(y_ps[k % 2][:, 0:D], hid_t[k % 2][:, c, :],
                                   w2[:, bass.ds(e, 1), c, :].rearrange("p a f -> p (a f)"),
                                   start=c == 0, stop=c == FC - 1)
                mm.then_inc(down_mm, 1)

            pe.sem_inc(up_mm, PAIR)
            pe.sem_inc(down_mm, PAIR)
            pe.wait_ge(table_done, 2)
            pe.wait_ge(w2_loaded, 16)
            turn_rows(0, 0, 0, 0)
            turn_rows(1, 0, 1, 1)
            up(0, 0)
            with pe.Fori(0, ROUNDS) as r:
                for j in range(RING):
                    up(r * RING + (j + 1), j + 1)
                    down(r * RING + j, j)
                    turn_rows(r * RING + (j + 2), r + (j + 2) // RING, (j + 2) % RING, j)
            for j in range(REST):
                i = ROUNDS * RING + j
                if j + 1 < REST:
                    up(i + 1, j + 1)
                down(i, j)
                if j + 2 < REST:
                    turn_rows(i + 2, ROUNDS, j + 2, j)

        @block.vector
        def _(dve):
            dve.wait_ge(dexp_done, 1)
            dve.tensor_scalar(dtmp[:, 1:2], dtmp[:, 0:1], 1.0, None, ALU.add).then_inc(sig, 1)
            dve.wait_ge(sig, 1)
            dve.reciprocal(dpow[:, 0:1], dtmp[:, 1:2]).then_inc(sig, 2)

            def spread(n, s, src):
                for t in tiles_of(s):
                    dve.bn_stats(st[n][:, t, :], src[:, t, :]).then_inc(stats_done[n], 1)

            def aggregate(n, s):
                dve.wait_ge(stats_done[n], CHUNKS * (s + 1))
                for t in tiles_of(s):
                    dve.bn_aggr(mv[n][:, t, :], st[n][:, t, :]).then_inc(aggr_done[n], 1)

            def widen(b):
                dve.wait_ge(dpow_done, b)
                dve.wait_ge(toep_done, b)
                src, sh = toep[b % 2], 1 << b
                dst = toep[(b + 1) % 2][:, P:] if b < 7 else decay_m[:, 0:2 * P]
                dve.scalar_tensor_tensor(out=dst, in0=src[:, P - sh:3 * P - sh], scalar=dpow[:, b:b + 1],
                                         in1=src[:, P:], op0=ALU.mult, op1=ALU.add) \
                    .then_inc(toep_done if b < 7 else decay_m_done, 1)

            dve.wait_ge(toep_start, 2)
            dve.wait_ge(sig, 3)
            widen(0)
            for s in range(2):
                dve.wait_ge(x_loaded[s], 16)
                for c in range(CHUNKS):
                    t = CHUNKS * s + c
                    dve.bn_stats(st[0][:, t, :], x[:, t, :]).then_inc(stats_done[0], 1)
                    if t < 7:
                        widen(1 + t)
                aggregate(0, s)
            for s in range(2, SEQS):
                dve.wait_ge(x_loaded[s], 16)
                spread(0, s, x)
                aggregate(0, s)

            def mix_in(s):
                dve.wait_ge(ret_mm, s + 1)
                dve.wait_ge(n1_done, CHUNKS * (s + 1))
                dve.tensor_tensor(out=mixed[:, of_seq(s), :], in0=ret_ps[s % 2][:].rearrange("p (c d) -> p c d", d=D),
                                  in1=n1[:, of_seq(s), :], op=ALU.add).then_inc(mixed_done, 1)
                dve.wait_ge(mixed_done, s + 1)
                yield
                spread(1, s, mixed)
                yield
                aggregate(1, s)

            def residual(s):
                dve.wait_ge(rstd_done[1], s + 1)
                for t in tiles_of(s):
                    dve.tensor_scalar(normed[:, t, :], mixed[:, t, :], mv[1][:, t, 0:1], rstd[1][:, t:t + 1],
                                      ALU.subtract, ALU.mult).then_inc(normed_done, 1)
                    yield
                dve.wait_ge(normed_done, CHUNKS * (s + 1))
                dve.tensor_tensor(out=x1[:, of_seq(s), :], in0=x[:, of_seq(s), :], in1=normed[:, of_seq(s), :],
                                  op=ALU.add).then_inc(x1_done, 1)
                yield
                dve.wait_ge(x1_done, s + 1)
                spread(2, s, x1)
                yield
                aggregate(2, s)

            rstep = [0]

            def step(instruction):
                rstep[0] += 1
                instruction.then_inc(router_step, 1)

            def settled():
                dve.wait_ge(router_step, rstep[0])

            full = [P, CHUNKS, E]

            def wide(v):
                return v.unsqueeze(2).broadcast_to(full)

            def route(s):
                dve.wait_ge(logits_mm, s + 1)
                dve.tensor_copy(lg[:], logit_ps).then_inc(logits_out, 1)
                dve.wait_ge(logits_out, s + 1)
                yield
                step(dve.tensor_reduce(out=lmax[:], in_=lg[:], axis=AX.X, op=ALU.max))
                for k, src, top in ((0, lg, lmax), (1, rest, second)):
                    yield
                    settled()
                    step(dve.tensor_tensor(out=tied[:], in0=src[:], in1=wide(top[:]), op=ALU.is_equal))
                    yield
                    if k == 0:
                        dve.tensor_tensor(out=ldif[:, :, 0:E], in0=lg[:], in1=wide(lmax[:]), op=ALU.subtract) \
                            .then_inc(ldif_done, 1)
                    else:
                        dve.tensor_tensor(out=ldif[:, :, E], in0=second[:], in1=lmax[:], op=ALU.subtract) \
                            .then_inc(ldif_done, 1)
                    settled()
                    step(dve.tensor_tensor(out=ranked[k][:], in0=tied[:], in1=prefer[:], op=ALU.mult))
                    yield
                    settled()
                    step(dve.tensor_reduce(out=best[k][:], in_=ranked[k][:], axis=AX.X, op=ALU.max))
                    yield
                    settled()
                    step(dve.tensor_tensor(out=pick[:, :, k, :], in0=ranked[k][:], in1=wide(best[k][:]),
                                           op=ALU.is_equal))
                    if k == 0:
                        yield
                        settled()
                        step(dve.scalar_tensor_tensor(out=rest[:], in0=pick[:, :, 0, :], scalar=LOWEST, in1=lg[:],
                                                      op0=ALU.mult, op1=ALU.add))
                        yield
                        settled()
                        step(dve.tensor_reduce(out=second[:], in_=rest[:], axis=AX.X, op=ALU.max))
                yield
                settled()
                dve.tensor_tensor(out=picks[:, s, :, :], in0=pick[:, :, 0, :], in1=pick[:, :, 1, :], op=ALU.add) \
                    .then_inc(picks_done, 1)
                step(dve.tensor_tensor(out=base[:], in0=count[:], in1=region_row[:], op=ALU.add))
                yield
                dve.wait_ge(exp_done, s + 1)
                step(dve.tensor_reduce(out=esum[:], in_=ex[:, :, 0:E], axis=AX.X, op=ALU.add))
                dve.wait_ge(rank_mm, s + 1)
                settled()
                step(dve.tensor_tensor(out=place[:], in0=rank_ps,
                                       in1=base[:].unsqueeze(1).broadcast_to(full), op=ALU.add))
                step(dve.reciprocal(einv[:], esum[:]))
                step(dve.tensor_tensor(out=count[:], in0=count[:], in1=total_ps, op=ALU.add))
                settled()
                step(dve.tensor_tensor(out=chosen[:], in0=pick[:], op=ALU.mult,
                                       in1=place[:].unsqueeze(2).broadcast_to([P, CHUNKS, K, E])))
                dve.tensor_copy(rows[:, of_seq(s), 0, GATE], einv[:]).then_inc(gates_done, 1)
                dve.tensor_tensor(out=rows[:, of_seq(s), 1, GATE], in0=ex[:, :, E], in1=einv[:], op=ALU.mult) \
                    .then_inc(gates_done, 1)
                settled()
                step(dve.tensor_reduce(out=slotf[:], in_=chosen[:], axis=AX.X, op=ALU.add))
                settled()
                dve.tensor_copy(slot_of[:, of_seq(s), :], slotf[:]).then_inc(slots_done, 1)
                yield

            def run(*parts):
                parts = list(parts)
                while parts:
                    parts = [p for p in parts if next(p, "ended") != "ended"]

            def chain(*parts):
                for p in parts:
                    yield from p

            run(mix_in(0))
            run(mix_in(1))
            run(residual(0))
            run(mix_in(2))
            run(residual(1))
            dve.wait_ge(router_consts, 7)
            run(route(0), chain(mix_in(3), residual(2)))
            run(route(1), residual(3))
            run(route(2))
            run(route(3))

            tstep = [0]

            def table(instruction):
                tstep[0] += 1
                instruction.then_inc(table_step, 1)
                dve.wait_ge(table_step, tstep[0])

            settled()
            dve.wait_ge(table_consts, 3)
            dve.tensor_tensor(out=pad_row[:], in0=count[:], in1=region_row[:], op=ALU.add).then_inc(pad_rows_done, 1)
            table(dve.tensor_scalar(cnt_i[:], count[:], float(P - 1), None, ALU.add))
            table(dve.tensor_single_scalar(nblk_i[:], cnt_i[:], 7, ALU.arith_shift_right))
            table(dve.tensor_copy(nblk[:], nblk_i[:]))
            table(dve.tensor_copy(cum[0][:, 4:], nblk[:]))
            for b in range(3):
                src, dst, sh = cum[b % 2], cum[(b + 1) % 2], 1 << b
                table(dve.tensor_tensor(out=dst[:, 4:], in0=src[:, 4:], in1=src[:, 4 - sh:4 - sh + E], op=ALU.add))
            by_block = [P, BLOCKS, E]
            table(dve.tensor_tensor(out=past[:], in0=cum[1][:, 4:].unsqueeze(1).broadcast_to(by_block),
                                    in1=step_no[:].unsqueeze(2).broadcast_to(by_block), op=ALU.is_le))
            table(dve.tensor_reduce(out=be[:], in_=past[:], axis=AX.X, op=ALU.add))
            dve.tensor_scalar(block_expert[:], be[:], float(E - 1), None, ALU.min).then_inc(table_done, 1)
            table(dve.tensor_tensor(out=pastn[:], in0=past[:], in1=nblk[:].unsqueeze(1).broadcast_to(by_block),
                                    op=ALU.mult))
            table(dve.tensor_reduce(out=bn[:], in_=pastn[:], axis=AX.X, op=ALU.add))
            table(dve.tensor_tensor(out=bt[:], in0=step_no[:], in1=bn[:], op=ALU.subtract))
            table(dve.tensor_scalar(bt[:], bt[:], float(P), None, ALU.mult))
            dve.scalar_tensor_tensor(out=block_row[:], in0=be[:], scalar=float(REGION), in1=bt[:],
                                     op0=ALU.mult, op1=ALU.add).then_inc(table_done, 1)

            dve.sem_inc(w1_ready, PAIR)
            dve.sem_inc(y_done, PAIR)
            dve.wait_ge(table_done, 2)
            dve.wait_ge(w1_loaded, 16)

            def fetch(i, k):
                e = dve.value_load(block_expert[0:1, bass.ds(i, 1)], min_val=0, max_val=E - 1)
                dve.wait_ge(up_mm, i + 1)
                dve.tensor_copy(w1_now[k % 2][:], w1[:, bass.ds(e, 1), :].rearrange("p a f -> p (a f)")) \
                    .then_inc(w1_ready, 1)

            def gated(i, r, j):
                dve.wait_ge(down_mm, i + 1 + PAIR)
                if r is not None:
                    dve.wait_ge(y_sent[j], r * 16)
                dve.tensor_scalar(y[j][:], y_ps[j % 2][:, 0:D], xg[j][:, GATE:GATE + 1], None, ALU.mult) \
                    .then_inc(y_done, 1)

            fetch(0, 0)
            fetch(1, 1)
            for j in range(RING):
                fetch(j + 2, j)
                gated(j, None, j)
            with dve.Fori(1, ROUNDS) as r:
                for j in range(RING):
                    fetch(r * RING + (j + 2), j)
                    gated(r * RING + j, r, j)
            for j in range(REST):
                if j + 2 < REST:
                    fetch(ROUNDS * RING + j + 2, j)
                gated(ROUNDS * RING + j, ROUNDS, j)

            for s in range(SEQS):
                dve.wait_ge(yk_loaded[s], 16)
                dve.tensor_tensor(out=n1[:, of_seq(s), :], in0=yk[:, of_seq(s), 0:D], in1=yk[:, of_seq(s), D:2 * D],
                                  op=ALU.add).then_inc(ff_done, 1)
                dve.wait_ge(ff_done, s + 1)
                spread(3, s, n1)
                aggregate(3, s)
            for s in range(SEQS):
                dve.wait_ge(fn_done, CHUNKS * (s + 1))
                dve.tensor_tensor(out=normed[:, of_seq(s), :], in0=mixed[:, of_seq(s), :], in1=x1[:, of_seq(s), :],
                                  op=ALU.add).then_inc(fo_done, 1)


def kernel(**inputs):
    import numpy as np
    import concourse.bacc as bacc
    from concourse.bass_utils import run_bass_kernel_spmd

    a = {n: np.asarray(v) for n, v in inputs.items()}
    back = (-np.arange(2 * P)) % P
    arrays = {
        "x_dram": np.ascontiguousarray(a["L0_attn_x"]),
        "keys_dram": np.stack([a["L0_attn_bind_key"][back], a["L0_attn_unbind_key"][back]]),
        "scalars_dram": np.ascontiguousarray(np.broadcast_to(
            np.concatenate([a["L0_attn_gate"].reshape(1), a["L0_attn_decay"].reshape(1)]), (P, 2))),
        "router_dram": np.ascontiguousarray(a["L0_ffn_router_w"]),
        "w1_dram": np.ascontiguousarray(a["L0_ffn_w1"]),
        "w2_dram": np.ascontiguousarray(a["L0_ffn_w2"]),
    }
    nc = bacc.Bacc("TRN2", target_bir_lowering=False, num_devices=1)
    aps = [nc.dram_tensor(n, v.shape, F32, kind="ExternalInput").ap() for n, v in arrays.items()]
    out = nc.dram_tensor("out_dram", (SEQS, SEQ, D), F32, kind="ExternalOutput").ap()
    slots = nc.dram_tensor("slots_dram", [E * REGION + SPARE * P, ROW], F32, kind="Internal").ap()
    returned = nc.dram_tensor("returned_dram", [K * TOKENS + (E + SPARE) * P, D], F32, kind="Internal").ap()
    build(nc, *aps, out, slots, returned)
    r = run_bass_kernel_spmd(nc, [arrays], core_ids=[0])
    return r.results[0]["out_dram"]
```

```python
from contextlib import ExitStack

import concourse.bass as bass
from concourse import mybir

P = 128
D = 128
SEQS, SEQ = 4, 512
TOKENS = SEQS * SEQ
TILES = TOKENS // P
CHUNKS = SEQ // P
E, F, K = 8, 512, 2
FC = F // P
EPS = 1e-5
WARMING = 14
WARMING_AGAIN = 12
RANKED_AFTER = 2
SENT_FIRST = 3
LOTS_PER_SEND = 2
LOWEST = -3e38
PIECES = ((0, 2), (2, 4), (4, 8), (8, 12), (12, 14), (14, 16))
ROOT_GUESS = 0x5f3759df

REGION = TOKENS + P
FULL_BLOCKS = K * TOKENS // P
BLOCKS = (K * TOKENS + E * (P - 1)) // P
RING = 8
EARLY_SEQS = (2, 3)
LATE = BLOCKS - len(EARLY_SEQS) * RING
SPARE = BLOCKS - FULL_BLOCKS
ROW = D + 2
ADDR, GATE = D, D + 1
ROUNDS = BLOCKS // RING
REST = BLOCKS - ROUNDS * RING
assert E == RING and SEQS == EARLY_SEQS[-1] + 1 and EARLY_SEQS[0] == 2
for _batch, _seqs in enumerate(EARLY_SEQS):
    assert (_batch + 1) * RING <= -(-(K * _seqs * SEQ - E * (P - 1)) // P)

F32 = mybir.dt.float32
I32 = mybir.dt.int32
BF16 = mybir.dt.bfloat16
ALU = mybir.AluOpType
ACT = mybir.ActivationFunctionType
AX = mybir.AxisListType


def build(nc, x_in, keys_in, scalars_in, router_in, w1_in, w2_in, out, slots, returned):
    ctx = ExitStack()
    with ctx:
        def sb(name, shape, dt=F32):
            return ctx.enter_context(nc.sbuf_tensor(name, shape, dt))

        def sem(name):
            return ctx.enter_context(nc.semaphore(name))

        x = sb("x", [P, TILES, D])
        n1 = sb("n1", [P, TILES, D])
        mixed = sb("mixed", [P, TILES, D])
        normed = sb("normed", [P, TILES, D])
        x1 = sb("x1", [P, TILES, D])
        holo_t = sb("holo_t", [P, SEQS, SEQ])
        n3_t = sb("n3_t", [P, SEQS, SEQ])
        rows = sb("rows", [P, TILES, K, ROW])
        n3 = rows[:, :, 0, 0:D]
        slot_of = sb("slot_of", [P, TILES, K], I32)
        w1 = sb("w1", [P, E, F])
        w2 = sb("w2", [P, E, FC, D])
        router = sb("router", [P, E])
        ident = sb("ident", [P, P])
        below = sb("below", [P, P], BF16)
        ones = sb("ones", [P, P], BF16)
        minus_half = sb("minus_half", [P, CHUNKS])
        prefer = sb("prefer", [P, CHUNKS, E])
        region_row = sb("region_row", [P, E])
        step_no = sb("step_no", [P, LATE])
        pads = sb("pads", [P, E + SPARE, ROW])
        scalars = sb("scalars", [P, 2])
        hankel = sb("hankel", [P, 2, P])
        mix = sb("mix", [P, P])
        dpow = sb("dpow", [P, 9])
        dtmp = sb("dtmp", [P, 2])
        toep = [sb(f"toep{i}", [P, 3 * P]) for i in range(2)]
        decay_m = sb("decay_m", [P, SEQ])
        st = [sb(f"st{n}", [P, TILES, 6]) for n in range(4)]
        mv = [sb(f"mv{n}", [P, TILES, 2]) for n in range(4)]
        ve = [sb(f"ve{n}", [P, TILES]) for n in range(4)]
        rstd = [sb(f"rstd{n}", [P, TILES]) for n in range(4)]
        neg_mean = [sb(f"neg_mean{n}", [P, TILES]) for n in range(4)]
        shift = [sb(f"shift{n}", [P, TILES]) for n in range(4)]
        ROOTS = ((3, 1), (2, 2), (3, 2))
        root_v = sb("root_v", [P, len(ROOTS), CHUNKS])
        root_bits = sb("root_bits", [P, len(ROOTS), CHUNKS], I32)
        root = sb("root", [P, len(ROOTS), 4, CHUNKS])
        root_sq = sb("root_sq", [P, len(ROOTS), 3, CHUNKS])
        root_dev = sb("root_dev", [P, len(ROOTS), 3, CHUNKS])
        lg = sb("lg", [P, CHUNKS, E])
        lmax = sb("lmax", [P, CHUNKS])
        second = sb("second", [P, CHUNKS])
        ldif = sb("ldif", [P, CHUNKS, E + 1])
        ex = sb("ex", [P, CHUNKS, E + 1])
        esum = sb("esum", [P, CHUNKS])
        einv = sb("einv", [P, CHUNKS])
        rest = sb("rest", [P, CHUNKS, E])
        tied = sb("tied", [P, CHUNKS, E])
        ranked = [sb(f"ranked{k}", [P, CHUNKS, E]) for k in range(K)]
        best = [sb(f"best{k}", [P, CHUNKS]) for k in range(K)]
        pick = sb("pick", [P, CHUNKS, K, E])
        picks = sb("picks", [P, SEQS, CHUNKS, E], BF16)
        count = sb("count", [P, E])
        base = sb("base", [P, E])
        place = sb("place", [P, CHUNKS, E])
        chosen = sb("chosen", [P, CHUNKS, K, E])
        slotf = sb("slotf", [P, CHUNKS, K])
        pad_row = sb("pad_row", [P, E], I32)
        cnt_i = sb("cnt_i", [P, E], I32)
        nblk_i = sb("nblk_i", [P, E], I32)
        nblk = sb("nblk", [P, E])
        cum = [sb(f"cum{i}", [P, 4 + E]) for i in range(2)]
        used = sb("used", [P, E + 1])
        taken = sb("taken", [P, E])
        taken_up_to = sb("taken_up_to", [P, E + 1])
        gone = sb("gone", [P, E])
        past = sb("past", [P, LATE, E])
        pastn = sb("pastn", [P, LATE, E])
        be = sb("be", [P, LATE])
        bn = sb("bn", [P, LATE])
        bt = sb("bt", [P, LATE])
        block_expert = sb("block_expert", [P, BLOCKS], I32)
        block_row = sb("block_row", [P, BLOCKS], I32)
        xg = [sb(f"xg{i}", [P, ROW]) for i in range(RING)]
        xg_t = [sb(f"xg_t{i}", [P, P]) for i in range(2)]
        w1_now = [sb(f"w1_now{i}", [P, F]) for i in range(2)]
        hid_t = [sb(f"hid_t{i}", [P, FC, P]) for i in range(2)]
        y = [sb(f"y{i}", [P, D]) for i in range(RING)]
        warm = sb("warm", [P, 1])
        yk = sb("yk", [P, TILES, K * D])

        bank = [ctx.enter_context(nc.psum_tensor(f"bank{i}", [P, 512], F32)) for i in range(8)]
        holo_ps, ret_ps, n3t_ps = bank[0:2], bank[2:4], bank[4:6]
        logit_ps = bank[6][:, 0:CHUNKS * E].rearrange("p (u e) -> p u e", e=E)
        mix_ps = bank[7][:, 0:P]
        rank_ps = bank[7][:, 0:CHUNKS * E].rearrange("p (u e) -> p u e", e=E)
        total_ps = bank[7][:, CHUNKS * E:CHUNKS * E + E]
        xgt_ps, up_ps, y_ps = bank[0:2], bank[2:4], bank[4:6]

        scalars_loaded = sem("scalars_loaded")
        keys_loaded = sem("keys_loaded")
        x_loaded = [sem(f"x_loaded{i}") for i in range(SEQS)]
        router_loaded = sem("router_loaded")
        w1_loaded = sem("w1_loaded")
        w2_loaded = sem("w2_loaded")
        zeroed = sem("zeroed")
        toep_start = sem("toep_start")
        ident_done = sem("ident_done")
        half_done = sem("half_done")
        router_consts = sem("router_consts")
        table_consts = sem("table_consts")
        sig = sem("sig")
        dexp_done = sem("dexp_done")
        dpow_done = sem("dpow_done")
        toep_done = sem("toep_done")
        decay_m_done = sem("decay_m_done")
        mix_mm = sem("mix_mm")
        mix_done = sem("mix_done")
        stats_done = [sem(f"stats_done{i}") for i in range(4)]
        aggr_done = [sem(f"aggr_done{i}") for i in range(4)]
        eps_added = [sem(f"eps_added{i}") for i in range(4)]
        rstd_done = [sem(f"rstd_done{i}") for i in range(4)]
        shift_done = [sem(f"shift_done{i}") for i in range(4)]
        root_step = [sem(f"root_step{i}") for i in range(len(ROOTS))]
        late_shift_done = sem("late_shift_done")
        n1_first = sem("n1_first")
        n1_done = sem("n1_done")
        holo_mm = sem("holo_mm")
        holo_out = sem("holo_out")
        ret_mm = sem("ret_mm")
        mixed_done = sem("mixed_done")
        normed_done = sem("normed_done")
        x1_done = sem("x1_done")
        n3_first = sem("n3_first")
        n3_done = sem("n3_done")
        n3t_mm = sem("n3t_mm")
        n3t_out = sem("n3t_out")
        rows_copied = sem("rows_copied")
        logits_mm = sem("logits_mm")
        logits_out = sem("logits_out")
        ldif_done = sem("ldif_done")
        exp_done = sem("exp_done")
        picks_done = sem("picks_done")
        rank_mm = sem("rank_mm")
        router_step = sem("router_step")
        slots_done = sem("slots_done")
        gates_done = sem("gates_done")
        dispatched = [sem(f"dispatched{i}") for i in range(3)]
        pads_ready = sem("pads_ready")
        spare_padded = sem("spare_padded")
        padded = sem("padded")
        pad_rows_done = sem("pad_rows_done")
        table_step = sem("table_step")
        table_done = [sem(f"table_done{i}") for i in range(3)]
        xg_loaded = [sem(f"xg_loaded{i}") for i in range(RING)]
        xgt_mm = sem("xgt_mm")
        xgt_out = sem("xgt_out")
        w1_ready = sem("w1_ready")
        up_mm = sem("up_mm")
        gelu_done = sem("gelu_done")
        down_mm = sem("down_mm")
        y_done = sem("y_done")
        sends = sem("sends")
        y_sent = [sem(f"y_sent{i}") for i in range(RING)]
        yk_loaded = [sem(f"yk_loaded{i}") for i in range(len(PIECES))]
        ff_done = sem("ff_done")
        fn_done = sem("fn_done")
        ff_normed = sem("ff_normed")
        fo_done = sem("fo_done")
        stored = sem("stored")

        block = ctx.enter_context(nc.Block())
        x_tiles = x_in.rearrange("s (c p) d -> s p c d", p=P)
        out_tiles = out.rearrange("s (c p) d -> s p c d", p=P)

        def of_seq(s):
            return slice(CHUNKS * s, CHUNKS * (s + 1))

        def tiles_of(s):
            return range(CHUNKS * s, CHUNKS * (s + 1))

        PAIR = 2

        def wait_normed(engine, first, done, s, tiles=CHUNKS):
            if s == 0:
                engine.wait_ge(first, tiles)
            else:
                engine.wait_ge(done, CHUNKS * (s - 1) + tiles)

        @block.sync
        def _(sp):
            sp.dma_start(scalars[:], scalars_in).then_inc(scalars_loaded, 16)
            for s in range(SEQS):
                sp.dma_start(x[:, of_seq(s), :], x_tiles[s]).then_inc(x_loaded[s], 16)
            sp.dma_start(router[:], router_in).then_inc(router_loaded, 16)
            sp.wait_ge(pads_ready, 2)
            sp.dma_start(slots[E * REGION:E * REGION + SPARE * P, :].rearrange("(b p) c -> p b c", p=P),
                         pads[:, E:, :]).then_inc(spare_padded, 16)

            def load_block(r, j):
                i = r * RING + j
                row = sp.value_load(block_row[0:1, bass.ds(i, 1)], min_val=0,
                                    max_val=E * REGION + (SPARE - 1) * P)
                if not isinstance(r, int) or r > 0:
                    sp.wait_ge(y_sent[j], r * 16)
                sp.dma_start(xg[j][:], slots[bass.ds(row, P), :]).then_inc(xg_loaded[j], 16)

            def pad(e):
                first = sp.value_load(pad_row[0:1, e:e + 1], min_val=0, max_val=E * REGION - P)
                sp.dma_start(slots[bass.ds(first, P), :], pads[:, e, :]).then_inc(padded, 16)

            sp.wait_ge(table_done[0], 2)
            sp.wait_ge(dispatched[0], 16 * 2 * CHUNKS * K)
            for j in range(RING):
                load_block(0, j)
            sp.wait_ge(table_done[1], 2)
            sp.wait_ge(dispatched[1], 16 * CHUNKS * K)
            load_block(1, 0)
            load_block(1, 1)
            sp.wait_ge(pad_rows_done, 1)
            pad(0)
            pad(1)
            for j in range(2, RING):
                pad(j)
                load_block(1, j)
            sp.wait_ge(table_done[2], 2)
            sp.wait_ge(spare_padded, 16)
            sp.wait_ge(padded, 16 * E)
            sp.wait_ge(dispatched[2], 16 * CHUNKS * K)
            with sp.Fori(2, ROUNDS) as r:
                for j in range(RING):
                    load_block(r, j)
            for j in range(REST):
                load_block(ROUNDS, j)
            for j in range(RING):
                sp.wait_ge(y_sent[j], 16 * (ROUNDS + (j < REST)))
            back = returned[0:K * TOKENS, :].rearrange("(t p k) d -> p t (k d)", p=P, k=K)
            for i, (first, end) in enumerate(PIECES):
                sp.dma_start(yk[:, first:end, :], back[:, first:end, :]).then_inc(yk_loaded[i], 16)
            for i, (first, end) in enumerate(PIECES):
                sp.wait_ge(fo_done, i + 1)
                s, c = divmod(first, CHUNKS)
                sp.dma_start(out_tiles[s][:, c:c + end - first, :], normed[:, first:end, :]).then_inc(stored, 16)
            sp.wait_ge(stored, 16 * len(PIECES))

        @block.gpsimd
        def _(pool):
            pool.memset(toep[0][:], 0.0).then_inc(zeroed, 1)
            pool.wait_ge(zeroed, 1)
            pool.affine_select(out=toep[0][:, P:], in_=toep[0][:, P:], compare_op=ALU.not_equal, fill=1.0, base=0,
                               pattern=[[-1, 2 * P]], channel_multiplier=1).then_inc(toep_start, 1)
            pool.memset(toep[1][:, 0:P], 0.0).then_inc(toep_start, 1)

            pool.memset(below[:], 1.0).then_inc(router_consts, 1)
            pool.memset(ones[:], 1.0).then_inc(router_consts, 1)
            pool.wait_ge(router_consts, 2)
            pool.affine_select(out=below[:], in_=below[:], compare_op=ALU.is_gt, fill=0.0, base=0,
                               pattern=[[1, P]], channel_multiplier=-1).then_inc(router_consts, 1)
            pool.iota(prefer[:], pattern=[[0, CHUNKS], [-1, E]], base=E, channel_multiplier=0,
                      allow_small_or_imprecise_dtypes=True).then_inc(router_consts, 1)
            pool.iota(region_row[:], pattern=[[REGION, E]], base=0, channel_multiplier=0,
                      allow_small_or_imprecise_dtypes=True).then_inc(router_consts, 1)
            pool.memset(count[:], 0.0).then_inc(router_consts, 1)
            pool.iota(rows[:, :, :, ADDR].bitcast(I32), pattern=[[K * P, TILES], [1, K]], base=0,
                      channel_multiplier=K).then_inc(router_consts, 1)
            pool.memset(minus_half[:], -0.5).then_inc(half_done, 1)
            pool.memset(ident[:], 0.0).then_inc(ident_done, 1)
            pool.wait_ge(ident_done, 1)
            pool.affine_select(out=ident[:], in_=ident[:], compare_op=ALU.not_equal, fill=1.0, base=0,
                               pattern=[[-1, P]], channel_multiplier=1).then_inc(ident_done, 1)

            pool.wait_ge(sig, 3)
            for b in range(8):
                if b:
                    pool.wait_ge(dpow_done, b)
                pool.tensor_tensor(out=dpow[:, b + 1:b + 2], in0=dpow[:, b:b + 1], in1=dpow[:, b:b + 1],
                                   op=ALU.mult).then_inc(dpow_done, 1)
            pool.wait_ge(half_done, 1)

            shifts = [0] * 4

            def one_over_std(s, n, with_shift):
                t = of_seq(s)
                shifts[n] += with_shift
                pool.wait_ge(aggr_done[n], CHUNKS * (s + 1))
                pool.tensor_scalar(ve[n][:, t], mv[n][:, t, 1], EPS, 1.0, ALU.add, ALU.mult).then_inc(eps_added[n], 1)
                if with_shift:
                    pool.tensor_scalar(neg_mean[n][:, t], mv[n][:, t, 0], -1.0, 0.0, ALU.mult, ALU.add) \
                        .then_inc(eps_added[n], 1)
                pool.wait_ge(eps_added[n], s + 1 + shifts[n])
                pool.tensor_tensor(out=rstd[n][:, t], in0=ve[n][:, t], in1=minus_half[:], op=ALU.pow) \
                    .then_inc(rstd_done[n], 1)
                if with_shift:
                    pool.wait_ge(rstd_done[n], s + 1)
                    pool.tensor_tensor(out=shift[n][:, t], in0=neg_mean[n][:, t], in1=rstd[n][:, t], op=ALU.mult) \
                        .then_inc(shift_done[n], 1)

            def dispatch(s, lots):
                pool.wait_ge(slots_done, s + 1)
                pool.wait_ge(gates_done, K * (s + 1))
                pool.wait_ge(rows_copied, s + 1)
                for c, k in lots:
                    t = CHUNKS * s + c
                    pool.indirect_dma_start(
                        out=slots, out_offset=bass.IndirectOffsetOnAxis(ap=slot_of[:, t, k:k + 1], axis=0),
                        in_=rows[:, t, k, :], in_offset=None).then_inc(dispatched[max(s - 1, 0)], 16)

            lots = [(c, k) for c in range(CHUNKS) for k in range(K)]
            one_over_std(0, 0, False)
            for s in range(1, SEQS):
                one_over_std(s, 0, True)
            one_over_std(0, 1, False)
            pool.memset(pads[:], 0.0).then_inc(pads_ready, 1)
            one_over_std(0, 2, False)
            one_over_std(1, 1, False)
            pool.wait_ge(pads_ready, 1)
            pool.iota(pads[:, :, ADDR].bitcast(I32), pattern=[[P, E + SPARE]], base=K * TOKENS,
                      channel_multiplier=1).then_inc(pads_ready, 1)
            pool.iota(step_no[:], pattern=[[1, LATE]], base=0, channel_multiplier=0,
                      allow_small_or_imprecise_dtypes=True).then_inc(table_consts, 1)
            for c in range(2):
                pool.memset(cum[c][:], 0.0).then_inc(table_consts, 1)
            pool.memset(used[:], 0.0).then_inc(table_consts, 1)
            pool.memset(taken_up_to[:], 0.0).then_inc(table_consts, 1)
            one_over_std(1, 2, True)
            one_over_std(2, 1, False)
            pool.wait_ge(router_consts, 7)
            dispatch(0, lots)
            dispatch(1, lots)
            dispatch(2, lots)

            def send(i, j):
                pool.wait_ge(y_done, i + 1 + PAIR)
                pool.sem_inc(sends, 1)
                pool.indirect_dma_start(
                    out=returned,
                    out_offset=bass.IndirectOffsetOnAxis(ap=xg[j][:, ADDR:ADDR + 1].bitcast(I32), axis=0),
                    in_=y[j][:], in_offset=None).then_inc(y_sent[j], 16)

            for j in range(SENT_FIRST):
                send(j, j)
            for j in range(SENT_FIRST, RING):
                dispatch(3, lots[LOTS_PER_SEND * (j - SENT_FIRST):LOTS_PER_SEND * (j - SENT_FIRST + 1)])
                send(j, j)
            with pool.Fori(1, ROUNDS) as r:
                for j in range(RING):
                    send(r * RING + j, j)
            for j in range(REST):
                send(ROUNDS * RING + j, j)
            for i, (first, end) in enumerate(PIECES):
                pool.wait_ge(aggr_done[3], end)
                pool.tensor_scalar(ve[3][:, first:end], mv[3][:, first:end, 1], EPS, 1.0, ALU.add, ALU.mult) \
                    .then_inc(eps_added[3], 1)
                last = i == len(PIECES) - 1
                if not last:
                    pool.tensor_scalar(neg_mean[3][:, first:end], mv[3][:, first:end, 0], -1.0, 0.0,
                                       ALU.mult, ALU.add).then_inc(eps_added[3], 1)
                pool.wait_ge(eps_added[3], 2 * (i + 1) - last)
                pool.tensor_tensor(out=rstd[3][:, first:end], in0=ve[3][:, first:end],
                                   in1=minus_half[:, 0:end - first], op=ALU.pow).then_inc(rstd_done[3], 1)
                if not last:
                    pool.wait_ge(rstd_done[3], i + 1)
                    pool.tensor_tensor(out=shift[3][:, first:end], in0=neg_mean[3][:, first:end],
                                       in1=rstd[3][:, first:end], op=ALU.mult).then_inc(shift_done[3], 1)

        @block.scalar
        def _(act):
            for k in range(2):
                act.dma_start(hankel[:, k, :], bass.AP(keys_in.tensor, 2 * P * k, [[1, P], [1, P]])) \
                    .then_inc(keys_loaded, 16)
            act.wait_ge(scalars_loaded, 16)
            act.activation(dtmp[:, 0:1], scalars[:, 1:2], ACT.Exp, scale=-1.0).then_inc(dexp_done, 1)
            act.wait_ge(mix_mm, 1)
            act.activation(mix[:], mix_ps, ACT.Copy, scale=scalars[:, 0:1]).then_inc(mix_done, 1)

            def normalise(s, n, dst, src, done, tiles=range(CHUNKS)):
                if (s, n) in ROOTS:
                    act.wait_ge(late_shift_done, s - 1)
                else:
                    act.wait_ge(shift_done[n], s)
                for t in tiles_of(s)[tiles.start:tiles.stop]:
                    act.activation(dst[:, t, :], src[:, t, :], ACT.Identity, bias=shift[n][:, t:t + 1],
                                   scale=rstd[n][:, t:t + 1]).then_inc(done, 1)

            def holo_copy(s):
                act.wait_ge(holo_mm, s + 1)
                act.activation(holo_t[:, s, :], holo_ps[s % 2][:], ACT.Copy).then_inc(holo_out, 1)

            def n3t_copy(s):
                act.wait_ge(n3t_mm, CHUNKS * (s + 1))
                act.activation(n3_t[:, s, :], n3t_ps[s % 2][:], ACT.Copy).then_inc(n3t_out, 1)

            def rows_copy(s):
                wait_normed(act, n3_first, n3_done, s)
                act.activation(rows[:, of_seq(s), 1, 0:D], n3[:, of_seq(s), :], ACT.Copy).then_inc(rows_copied, 1)

            def exps(s):
                act.wait_ge(ldif_done, 2 * (s + 1))
                act.activation(ex[:], ldif[:], ACT.Exp).then_inc(exp_done, 1)

            act.wait_ge(decay_m_done, 1)
            act.wait_ge(dpow_done, 8)
            for c in range(2, CHUNKS):
                act.activation(decay_m[:, P * c:P * (c + 1)], decay_m[:, P:2 * P], ACT.Copy,
                               scale=dpow[:, 5 + c:6 + c]).then_inc(decay_m_done, 1)
            normalise(1, 0, n1, x, n1_done, range(0, 2))
            holo_copy(0)
            normalise(1, 0, n1, x, n1_done, range(2, CHUNKS))
            normalise(2, 0, n1, x, n1_done)
            holo_copy(1)
            normalise(3, 0, n1, x, n1_done)
            holo_copy(2)
            holo_copy(3)
            act.dma_start(w1[:], w1_in.rearrange("e d f -> d e f")).then_inc(w1_loaded, 16)
            act.dma_start(w2[:], w2_in.rearrange("e (c f) d -> f e c d", f=P)).then_inc(w2_loaded, 16)
            for s in range(SEQS - 1):
                if s:
                    normalise(s, 2, n3, x1, n3_done)
                n3t_copy(s)
                rows_copy(s)
                exps(s)

            act.sem_inc(xgt_out, PAIR)
            act.sem_inc(gelu_done, PAIR)

            def rows_out(i, k):
                act.wait_ge(xgt_mm, i + 1)
                act.wait_ge(up_mm, i + 1)
                act.activation(xg_t[k % 2][:], xgt_ps[k % 2][:, 0:P], ACT.Copy).then_inc(xgt_out, 1)

            def gelu(i, k):
                act.wait_ge(up_mm, i + 1 + PAIR)
                act.wait_ge(down_mm, i + 1)
                act.activation(hid_t[k % 2][:].rearrange("p c t -> p (c t)"), up_ps[k % 2][:],
                               ACT.Gelu_apprx_tanh).then_inc(gelu_done, 1)

            normalise(3, 2, n3, x1, n3_done)
            rows_out(0, 0)
            rows_out(1, 1)
            n3t_copy(3)
            act.activation(warm[:], scalars[:, 0:1], ACT.Gelu_apprx_tanh)
            gelu(0, 0)
            rows_copy(3)
            for j in range(RING):
                if j == RANKED_AFTER:
                    exps(3)
                rows_out(j + 2, j)
                gelu(j + 1, j + 1)
            with act.Fori(1, ROUNDS) as r:
                for j in range(RING):
                    rows_out(r * RING + (j + 2), j)
                    gelu(r * RING + (j + 1), j + 1)
            for j in range(REST):
                if j + 2 < REST:
                    rows_out(ROUNDS * RING + j + 2, j)
                if j + 1 < REST:
                    gelu(ROUNDS * RING + j + 1, j + 1)
            for i, (first, end) in enumerate(PIECES[:-1]):
                act.wait_ge(shift_done[3], i + 1)
                for t in range(first, end):
                    act.activation(mixed[:, t, :], n1[:, t, :], ACT.Identity, bias=shift[3][:, t:t + 1],
                                   scale=rstd[3][:, t:t + 1]).then_inc(fn_done, 1)

        @block.tensor
        def _(pe):
            pe.sem_inc(up_mm, PAIR)
            pe.sem_inc(down_mm, PAIR)
            pe.wait_ge(keys_loaded, 32)
            pe.matmul(mix_ps, hankel[:, 0, :], hankel[:, 1, :], start=True, stop=True).then_inc(mix_mm, 1)
            def warm_up(products):
                for _ in range(products):
                    pe.matmul(bank[5][:, 0:P], hankel[:, 0, :], hankel[:, 1, :], start=True, stop=True)

            warm_up(WARMING)
            pe.wait_ge(decay_m_done, CHUNKS - 1)

            def hologram(s):
                if s >= 2:
                    pe.wait_ge(holo_out, s - 1)
                for c in range(CHUNKS):
                    wait_normed(pe, n1_first, n1_done, s, c + 1)
                    mm = pe.matmul(holo_ps[s % 2][:, P * c:SEQ], n1[:, CHUNKS * s + c, :],
                                   decay_m[:, 0:SEQ - P * c], start=c == 0, stop=c == CHUNKS - 1)
                mm.then_inc(holo_mm, 1)

            def retrieve(s):
                pe.wait_ge(holo_out, s + 1)
                if s >= 2:
                    pe.wait_ge(mixed_done, s - 1)
                for c in range(CHUNKS):
                    mm = pe.matmul(ret_ps[s % 2][:, P * c:P * (c + 1)], holo_t[:, s, P * c:P * (c + 1)], mix[:],
                                   start=True, stop=True)
                mm.then_inc(ret_mm, 1)

            def turn_tokens(s):
                for c in range(CHUNKS):
                    wait_normed(pe, n3_first, n3_done, s, c + 1)
                    pe.transpose(n3t_ps[s % 2][:, P * c:P * (c + 1)], n3[:, CHUNKS * s + c, :], ident[:]) \
                        .then_inc(n3t_mm, 1)

            def logits(s):
                if s:
                    pe.wait_ge(logits_out, s)
                pe.wait_ge(n3t_out, s + 1)
                for c in range(CHUNKS):
                    mm = pe.matmul(logit_ps[:, c, :], n3_t[:, s, P * c:P * (c + 1)], router[:],
                                   start=True, stop=True)
                mm.then_inc(logits_mm, 1)

            def ranks(s):
                pe.wait_ge(picks_done, s + 1)
                pe.matmul(rank_ps, below[:], picks[:, s, :, :], start=True, stop=False)
                for c in range(CHUNKS - 1):
                    pe.matmul(rank_ps[:, c + 1:, :], ones[:],
                              picks[:, s, c:c + 1, :].broadcast_to([P, CHUNKS - 1 - c, E]),
                              start=False, stop=c == CHUNKS - 2)
                for c in range(CHUNKS):
                    mm = pe.matmul(total_ps, ones[:], picks[:, s, c, :], start=c == 0, stop=c == CHUNKS - 1)
                mm.then_inc(rank_mm, 1)

            pe.wait_ge(mix_done, 1)
            hologram(0)
            retrieve(0)
            hologram(1)
            hologram(2)
            retrieve(1)
            hologram(3)
            retrieve(2)
            retrieve(3)
            pe.wait_ge(ident_done, 2)
            pe.wait_ge(router_loaded, 16)
            pe.wait_ge(router_consts, 7)
            for s in range(SEQS - 1):
                turn_tokens(s)
                logits(s)
                ranks(s)

            def turn_rows(i, r, j, k):
                pe.wait_ge(xg_loaded[j], r * 16 + 16)
                pe.wait_ge(xgt_out, i + 1)
                pe.transpose(xgt_ps[k % 2][:, 0:P], xg[j][:, 0:D], ident[:]).then_inc(xgt_mm, 1)

            def up(i, k):
                pe.wait_ge(w1_ready, i + 1 + PAIR)
                pe.wait_ge(xgt_out, i + 1 + PAIR)
                pe.wait_ge(gelu_done, i + 1)
                for c in range(FC):
                    mm = pe.matmul(up_ps[k % 2][:, P * c:P * (c + 1)], w1_now[k % 2][:, P * c:P * (c + 1)],
                                   xg_t[k % 2][:], start=True, stop=True)
                mm.then_inc(up_mm, 1)

            def expert_of(i):
                return pe.value_load(block_expert[0:1, bass.ds(i, 1)], min_val=0, max_val=E - 1)

            def down(i, k, e):
                pe.wait_ge(gelu_done, i + 1 + PAIR)
                pe.wait_ge(y_done, i + 1)
                for c in range(FC):
                    mm = pe.matmul(y_ps[k % 2][:, 0:D], hid_t[k % 2][:, c, :],
                                   w2[:, bass.ds(e, 1), c, :].rearrange("p a f -> p (a f)"),
                                   start=c == 0, stop=c == FC - 1)
                mm.then_inc(down_mm, 1)

            def step(r, j):
                e = expert_of(r * RING + j)
                turn_rows(r * RING + (j + 2), r + (j + 2) // RING, (j + 2) % RING, j)
                up(r * RING + (j + 1), j + 1)
                down(r * RING + j, j, e)

            warm_up(WARMING_AGAIN)
            pe.wait_ge(table_done[0], 2)
            pe.wait_ge(w2_loaded, 16)
            turn_rows(0, 0, 0, 0)
            turn_rows(1, 0, 1, 1)
            turn_tokens(3)
            up(0, 0)
            logits(3)
            for j in range(RING):
                if j == RANKED_AFTER:
                    ranks(3)
                step(0, j)
            with pe.Fori(1, ROUNDS) as r:
                for j in range(RING):
                    step(r, j)
            for j in range(REST):
                i = ROUNDS * RING + j
                e = expert_of(i)
                if j + 2 < REST:
                    turn_rows(i + 2, ROUNDS, j + 2, j)
                if j + 1 < REST:
                    up(i + 1, j + 1)
                down(i, j, e)

        @block.vector
        def _(dve):
            dve.wait_ge(dexp_done, 1)
            dve.tensor_scalar(dtmp[:, 1:2], dtmp[:, 0:1], 1.0, None, ALU.add).then_inc(sig, 1)
            dve.wait_ge(sig, 1)
            dve.reciprocal(dpow[:, 0:1], dtmp[:, 1:2]).then_inc(sig, 2)

            def spread(n, s, src):
                for t in tiles_of(s):
                    dve.bn_stats(st[n][:, t, :], src[:, t, :]).then_inc(stats_done[n], 1)

            def aggregate(n, s):
                dve.wait_ge(stats_done[n], CHUNKS * (s + 1))
                for t in tiles_of(s):
                    dve.bn_aggr(mv[n][:, t, :], st[n][:, t, :]).then_inc(aggr_done[n], 1)

            def normalise(s, n, dst, src, done):
                dve.wait_ge(rstd_done[n], s + 1)
                for t in tiles_of(s):
                    dve.tensor_scalar(dst[:, t, :], src[:, t, :], mv[n][:, t, 0:1], rstd[n][:, t:t + 1],
                                      ALU.subtract, ALU.mult).then_inc(done, 1)

            def widen(b):
                dve.wait_ge(dpow_done, b)
                dve.wait_ge(toep_done, b)
                src, sh = toep[b % 2], 1 << b
                dst = toep[(b + 1) % 2][:, P:] if b < 7 else decay_m[:, 0:2 * P]
                dve.scalar_tensor_tensor(out=dst, in0=src[:, P - sh:3 * P - sh], scalar=dpow[:, b:b + 1],
                                         in1=src[:, P:], op0=ALU.mult, op1=ALU.add) \
                    .then_inc(toep_done if b < 7 else decay_m_done, 1)

            dve.wait_ge(toep_start, 2)
            dve.wait_ge(sig, 3)
            widen(0)
            for s in range(2):
                dve.wait_ge(x_loaded[s], 16)
                for c in range(CHUNKS):
                    t = CHUNKS * s + c
                    dve.bn_stats(st[0][:, t, :], x[:, t, :]).then_inc(stats_done[0], 1)
                    if t < 7:
                        widen(1 + t)
                if s:
                    normalise(0, 0, n1, x, n1_first)
                aggregate(0, s)
            for s in range(2, SEQS):
                dve.wait_ge(x_loaded[s], 16)
                spread(0, s, x)
                aggregate(0, s)

            def mix_in(s):
                dve.wait_ge(ret_mm, s + 1)
                wait_normed(dve, n1_first, n1_done, s)
                dve.tensor_tensor(out=mixed[:, of_seq(s), :], in0=ret_ps[s % 2][:].rearrange("p (c d) -> p c d", d=D),
                                  in1=n1[:, of_seq(s), :], op=ALU.add).then_inc(mixed_done, 1)
                dve.wait_ge(mixed_done, s + 1)
                for t in tiles_of(s):
                    yield
                    dve.bn_stats(st[1][:, t, :], mixed[:, t, :]).then_inc(stats_done[1], 1)
                yield
                aggregate(1, s)

            ROOT_STEPS = 3 + 3 * 3

            def one_over_std(s, n):
                m, t = ROOTS.index((s, n)), of_seq(s)
                done = root_step[m]
                steps = [0]

                def then(instruction):
                    steps[0] += 1
                    instruction.then_inc(done, 1)
                    yield
                    dve.wait_ge(done, steps[0])

                dve.wait_ge(aggr_done[n], CHUNKS * (s + 1))
                yield from then(dve.tensor_scalar(root_v[:, m, :], mv[n][:, t, 1], EPS, None, ALU.add))
                yield from then(dve.tensor_single_scalar(root_bits[:, m, :], root_v[:, m, :].bitcast(I32), 1,
                                                         ALU.arith_shift_right))
                yield from then(dve.tensor_scalar(root[:, m, 0, :].bitcast(I32), root_bits[:, m, :], -1.0,
                                                  float(ROOT_GUESS),
                                                  ALU.mult, ALU.add))
                for b in range(3):
                    y_now = root[:, m, b, :]
                    y_next = root[:, m, b + 1, :] if b < 2 else rstd[n][:, t]
                    yield from then(dve.tensor_tensor(out=root_sq[:, m, b, :], in0=y_now, in1=y_now, op=ALU.mult))
                    yield from then(dve.scalar_tensor_tensor(out=root_dev[:, m, b, :], in0=root_sq[:, m, b, :],
                                                             scalar=-0.5,
                                                             in1=root_v[:, m, :], op0=ALU.mult, op1=ALU.mult))
                    yield from then(dve.scalar_tensor_tensor(out=y_next, in0=root_dev[:, m, b, :], scalar=1.5,
                                                             in1=y_now,
                                                             op0=ALU.add, op1=ALU.mult))
                if n == 2:
                    dve.scalar_tensor_tensor(out=shift[n][:, t], in0=mv[n][:, t, 0], scalar=-1.0, in1=rstd[n][:, t],
                                             op0=ALU.mult, op1=ALU.mult).then_inc(late_shift_done, 1)
                    yield

            def residual(s):
                if (s, 1) in ROOTS:
                    dve.wait_ge(root_step[ROOTS.index((s, 1))], ROOT_STEPS)
                else:
                    dve.wait_ge(rstd_done[1], s + 1)
                for t in tiles_of(s):
                    dve.tensor_scalar(normed[:, t, :], mixed[:, t, :], mv[1][:, t, 0:1], rstd[1][:, t:t + 1],
                                      ALU.subtract, ALU.mult).then_inc(normed_done, 1)
                    yield
                dve.wait_ge(normed_done, CHUNKS * (s + 1))
                dve.tensor_tensor(out=x1[:, of_seq(s), :], in0=x[:, of_seq(s), :], in1=normed[:, of_seq(s), :],
                                  op=ALU.add).then_inc(x1_done, 1)
                yield
                dve.wait_ge(x1_done, s + 1)
                for t in tiles_of(s):
                    dve.bn_stats(st[2][:, t, :], x1[:, t, :]).then_inc(stats_done[2], 1)
                    yield
                aggregate(2, s)

            rstep = [0]

            def step(instruction):
                rstep[0] += 1
                instruction.then_inc(router_step, 1)

            def settled():
                dve.wait_ge(router_step, rstep[0])

            full = [P, CHUNKS, E]

            def wide(v):
                return v.unsqueeze(2).broadcast_to(full)

            def route(s):
                dve.wait_ge(logits_mm, s + 1)
                dve.tensor_copy(lg[:], logit_ps).then_inc(logits_out, 1)
                dve.wait_ge(logits_out, s + 1)
                yield
                step(dve.tensor_reduce(out=lmax[:], in_=lg[:], axis=AX.X, op=ALU.max))
                for k, src, top in ((0, lg, lmax), (1, rest, second)):
                    yield
                    settled()
                    step(dve.tensor_tensor(out=tied[:], in0=src[:], in1=wide(top[:]), op=ALU.is_equal))
                    yield
                    if k == 0:
                        dve.tensor_tensor(out=ldif[:, :, 0:E], in0=lg[:], in1=wide(lmax[:]), op=ALU.subtract) \
                            .then_inc(ldif_done, 1)
                    else:
                        dve.tensor_tensor(out=ldif[:, :, E], in0=second[:], in1=lmax[:], op=ALU.subtract) \
                            .then_inc(ldif_done, 1)
                    settled()
                    step(dve.tensor_tensor(out=ranked[k][:], in0=tied[:], in1=prefer[:], op=ALU.mult))
                    yield
                    settled()
                    step(dve.tensor_reduce(out=best[k][:], in_=ranked[k][:], axis=AX.X, op=ALU.max))
                    yield
                    settled()
                    step(dve.tensor_tensor(out=pick[:, :, k, :], in0=ranked[k][:], in1=wide(best[k][:]),
                                           op=ALU.is_equal))
                    if k == 0:
                        yield
                        settled()
                        step(dve.scalar_tensor_tensor(out=rest[:], in0=pick[:, :, 0, :], scalar=LOWEST, in1=lg[:],
                                                      op0=ALU.mult, op1=ALU.add))
                        yield
                        settled()
                        step(dve.tensor_reduce(out=second[:], in_=rest[:], axis=AX.X, op=ALU.max))
                yield
                settled()
                dve.tensor_tensor(out=picks[:, s, :, :], in0=pick[:, :, 0, :], in1=pick[:, :, 1, :], op=ALU.add) \
                    .then_inc(picks_done, 1)
                step(dve.tensor_tensor(out=base[:], in0=count[:], in1=region_row[:], op=ALU.add))
                yield
                dve.wait_ge(exp_done, s + 1)
                step(dve.tensor_reduce(out=esum[:], in_=ex[:, :, 0:E], axis=AX.X, op=ALU.add))
                yield
                dve.wait_ge(rank_mm, s + 1)
                settled()
                step(dve.tensor_tensor(out=place[:], in0=rank_ps,
                                       in1=base[:].unsqueeze(1).broadcast_to(full), op=ALU.add))
                step(dve.reciprocal(einv[:], esum[:]))
                step(dve.tensor_tensor(out=count[:], in0=count[:], in1=total_ps, op=ALU.add))
                settled()
                step(dve.tensor_tensor(out=chosen[:], in0=pick[:], op=ALU.mult,
                                       in1=place[:].unsqueeze(2).broadcast_to([P, CHUNKS, K, E])))
                dve.tensor_copy(rows[:, of_seq(s), 0, GATE], einv[:]).then_inc(gates_done, 1)
                dve.tensor_tensor(out=rows[:, of_seq(s), 1, GATE], in0=ex[:, :, E], in1=einv[:], op=ALU.mult) \
                    .then_inc(gates_done, 1)
                settled()
                step(dve.tensor_reduce(out=slotf[:], in_=chosen[:], axis=AX.X, op=ALU.add))
                settled()
                dve.tensor_copy(slot_of[:, of_seq(s), :], slotf[:]).then_inc(slots_done, 1)
                yield

            def run(*parts):
                parts = list(parts)
                while parts:
                    parts = [p for p in parts if next(p, "ended") != "ended"]

            def chain(*parts):
                for p in parts:
                    yield from p

            def some(part, steps):
                for _ in range(steps):
                    next(part)

            run(mix_in(0))
            run(residual(0))
            mix_1, mix_2, residual_1 = mix_in(1), mix_in(2), residual(1)
            some(mix_1, 5)
            normalise(0, 2, n3, x1, n3_first)
            run(mix_1)
            some(mix_2, 1)
            some(residual_1, 3)
            dve.wait_ge(router_consts, 7)
            run(route(0), chain(residual_1, mix_2))
            tstep = [0]

            def table(instruction):
                tstep[0] += 1
                instruction.then_inc(table_step, 1)
                yield
                dve.wait_ge(table_step, tstep[0])

            def running_sums():
                yield from table(dve.tensor_copy(cum[0][:, 4:], nblk[:]))
                for b in range(3):
                    src, dst, sh = cum[b % 2], cum[(b + 1) % 2], 1 << b
                    yield from table(dve.tensor_tensor(out=dst[:, 4:], in0=src[:, 4:], in1=src[:, 4 - sh:4 - sh + E],
                                                       op=ALU.add))

            def fill_table(first, blocks, done):
                by_block = [P, blocks, E]
                yield from table(dve.tensor_tensor(out=past[:, 0:blocks, :],
                                                   in0=cum[1][:, 4:].unsqueeze(1).broadcast_to(by_block),
                                                   in1=step_no[:, 0:blocks].unsqueeze(2).broadcast_to(by_block),
                                                   op=ALU.is_le))
                yield from table(dve.tensor_reduce(out=be[:, 0:blocks], in_=past[:, 0:blocks, :], axis=AX.X,
                                                   op=ALU.add))
                dve.tensor_scalar(block_expert[:, first:first + blocks], be[:, 0:blocks], float(E - 1), None,
                                  ALU.min).then_inc(done, 1)
                yield from table(dve.tensor_tensor(out=pastn[:, 0:blocks, :], in0=past[:, 0:blocks, :],
                                                   in1=gone[:].unsqueeze(1).broadcast_to(by_block), op=ALU.mult))
                yield from table(dve.tensor_reduce(out=bn[:, 0:blocks], in_=pastn[:, 0:blocks, :], axis=AX.X,
                                                   op=ALU.add))
                yield from table(dve.scalar_tensor_tensor(out=bt[:, 0:blocks], in0=step_no[:, 0:blocks],
                                                          scalar=used[:, 0:1],
                                                          in1=bn[:, 0:blocks], op0=ALU.add, op1=ALU.subtract))
                yield from table(dve.tensor_scalar(bt[:, 0:blocks], bt[:, 0:blocks], float(P), None, ALU.mult))
                dve.scalar_tensor_tensor(out=block_row[:, first:first + blocks], in0=be[:, 0:blocks],
                                         scalar=float(REGION), in1=bt[:, 0:blocks], op0=ALU.mult, op1=ALU.add) \
                    .then_inc(done, 1)
                yield

            def batch_table(batch):
                last = batch == len(EARLY_SEQS)
                first = batch * RING
                settled()
                dve.wait_ge(table_consts, 5)
                if last:
                    dve.tensor_tensor(out=pad_row[:], in0=count[:], in1=region_row[:], op=ALU.add) \
                        .then_inc(pad_rows_done, 1)
                yield from table(dve.tensor_scalar(cnt_i[:], count[:], float(P - 1) if last else 0.0, None, ALU.add))
                yield from table(dve.tensor_single_scalar(nblk_i[:], cnt_i[:], 7, ALU.arith_shift_right))
                yield from table(dve.tensor_tensor(out=nblk[:], in0=nblk_i[:], in1=used[:, 0:E], op=ALU.subtract))
                yield from table(dve.tensor_tensor(out=gone[:], in0=nblk[:], in1=used[:, 0:E], op=ALU.add))
                yield from table(dve.tensor_tensor(out=gone[:], in0=gone[:], in1=used[:, 1:], op=ALU.subtract))
                yield from running_sums()
                yield from fill_table(first, LATE if last else RING, table_done[batch])
                if not last:
                    dve.wait_ge(table_done[batch], 2)
                    yield from table(dve.tensor_scalar(taken_up_to[:, 1:], cum[1][:, 4:], float(RING), None, ALU.min))
                    yield from table(dve.tensor_tensor(out=taken[:], in0=taken_up_to[:, 1:], in1=taken_up_to[:, 0:E],
                                                       op=ALU.subtract))
                    yield from table(dve.tensor_tensor(out=used[:, 0:E], in0=used[:, 0:E], in1=taken[:], op=ALU.add))

            def fetch(i, k):
                e = dve.value_load(block_expert[0:1, bass.ds(i, 1)], min_val=0, max_val=E - 1)
                dve.wait_ge(up_mm, i + 1)
                dve.tensor_copy(w1_now[k % 2][:], w1[:, bass.ds(e, 1), :].rearrange("p a f -> p (a f)")) \
                    .then_inc(w1_ready, 1)

            def gated(i, r, j):
                dve.wait_ge(down_mm, i + 1 + PAIR)
                if r is not None:
                    dve.wait_ge(y_sent[j], r * 16)
                dve.tensor_scalar(y[j][:], y_ps[j % 2][:, 0:D], xg[j][:, GATE:GATE + 1], None, ALU.mult) \
                    .then_inc(y_done, 1)

            def blocks(js, pause):
                for j in js:
                    if j:
                        fetch(j + 2, j)
                    for _ in range(pause):
                        yield
                    gated(j, None, j)
                    for _ in range(pause):
                        yield

            run(residual(2))
            run(route(1), chain(one_over_std(2, 2), mix_in(3)))
            first_table = batch_table(0)
            run(one_over_std(3, 1), (next(first_table) for _ in range(12)))
            run(route(2), chain(first_table, residual(3), one_over_std(3, 2)))
            dve.sem_inc(w1_ready, PAIR)
            dve.sem_inc(y_done, PAIR)
            dve.wait_ge(w1_loaded, 16)
            second_table = batch_table(1)
            fetch(0, 0)
            fetch(1, 1)
            some(second_table, 8)
            fetch(2, 2)
            run(route(3), blocks(range(RANKED_AFTER), 6), second_table)
            run(blocks(range(RANKED_AFTER, RING), 2), batch_table(2))

            dve.wait_ge(table_done[2], 2)
            with dve.Fori(1, ROUNDS) as r:
                for j in range(RING):
                    fetch(r * RING + (j + 2), j)
                    gated(r * RING + j, r, j)
            for j in range(REST):
                if j + 2 < REST:
                    fetch(ROUNDS * RING + j + 2, j)
                gated(ROUNDS * RING + j, ROUNDS, j)

            for i, (first, end) in enumerate(PIECES):
                dve.wait_ge(yk_loaded[i], 16)
                dve.tensor_tensor(out=n1[:, first:end, :], in0=yk[:, first:end, 0:D], in1=yk[:, first:end, D:2 * D],
                                  op=ALU.add).then_inc(ff_done, 1)
                dve.wait_ge(ff_done, i + 1)
                for t in range(first, end):
                    dve.bn_stats(st[3][:, t, :], n1[:, t, :]).then_inc(stats_done[3], 1)
                dve.wait_ge(stats_done[3], end)
                for t in range(first, end):
                    dve.bn_aggr(mv[3][:, t, :], st[3][:, t, :]).then_inc(aggr_done[3], 1)
            for i, (first, end) in enumerate(PIECES):
                if i < len(PIECES) - 1:
                    dve.wait_ge(fn_done, end)
                else:
                    dve.wait_ge(rstd_done[3], i + 1)
                    for t in range(first, end):
                        dve.tensor_scalar(mixed[:, t, :], n1[:, t, :], mv[3][:, t, 0:1], rstd[3][:, t:t + 1],
                                          ALU.subtract, ALU.mult).then_inc(ff_normed, 1)
                    dve.wait_ge(ff_normed, end - first)
                dve.tensor_tensor(out=normed[:, first:end, :], in0=mixed[:, first:end, :], in1=x1[:, first:end, :],
                                  op=ALU.add).then_inc(fo_done, 1)


def kernel(**inputs):
    import numpy as np
    import concourse.bacc as bacc
    from concourse.bass_utils import run_bass_kernel_spmd

    a = {n: np.asarray(v) for n, v in inputs.items()}
    back = (-np.arange(2 * P)) % P
    arrays = {
        "x_dram": np.ascontiguousarray(a["L0_attn_x"]),
        "keys_dram": np.stack([a["L0_attn_bind_key"][back], a["L0_attn_unbind_key"][back]]),
        "scalars_dram": np.ascontiguousarray(np.broadcast_to(
            np.concatenate([a["L0_attn_gate"].reshape(1), a["L0_attn_decay"].reshape(1)]), (P, 2))),
        "router_dram": np.ascontiguousarray(a["L0_ffn_router_w"]),
        "w1_dram": np.ascontiguousarray(a["L0_ffn_w1"]),
        "w2_dram": np.ascontiguousarray(a["L0_ffn_w2"]),
    }
    nc = bacc.Bacc("TRN2", target_bir_lowering=False, num_devices=1)
    aps = [nc.dram_tensor(n, v.shape, F32, kind="ExternalInput").ap() for n, v in arrays.items()]
    out = nc.dram_tensor("out_dram", (SEQS, SEQ, D), F32, kind="ExternalOutput").ap()
    slots = nc.dram_tensor("slots_dram", [E * REGION + SPARE * P, ROW], F32, kind="Internal").ap()
    returned = nc.dram_tensor("returned_dram", [K * TOKENS + (E + SPARE) * P, D], F32, kind="Internal").ap()
    build(nc, *aps, out, slots, returned)
    r = run_bass_kernel_spmd(nc, [arrays], core_ids=[0])
    return r.results[0]["out_dram"]
```
